# Optimizing a Trainium2 kernel written in Bass

```python
import numpy as np
import jax
import jax.numpy as jnp

def _softmax(x, axis=-1):
    return jax.nn.softmax(x, axis=axis)

def _gelu(x):
    return jax.nn.gelu(x, approximate=True)

def _silu(x):
    return jax.nn.silu(x)

def _sigmoid(x):
    return jax.nn.sigmoid(x)

def _layernorm(x, axis=-1, eps=1e-05):
    m = jnp.mean(x, axis=axis, keepdims=True)
    v = jnp.var(x, axis=axis, keepdims=True)
    return (x - m) / jnp.sqrt(v + eps)

def _scatter_add(tgt, idx, src, axis=0):
    return tgt.at[idx].add(src)

def _segment_sum(src, seg, n):
    return jax.ops.segment_sum(src, seg, n)
kernel_name = 'mk_adaln_d1_jaxref_r2_dcf314'

def setup_inputs(seed: int=0):
    np.random.seed(seed)
    _w = jnp.asarray

    def _L0_attn_setup():
        import jax, jax.numpy as jnp
        import numpy as np
        B, N, D, H = (4, 2048, 512, 16)
        GN_EPS = 0.00064
        key = jax.random.key(seed)
        ks = jax.random.split(key, 12)
        x = jax.random.normal(ks[0], (B, N, D), jnp.float32)
        ddd = jnp.linspace(0.0, 1.0, D).reshape(1, 1, D)
        s = 1.0 / np.sqrt(D)
        w = lambda k: jax.random.normal(k, (D, D), jnp.float32) * s
        return {'x': x, 'x_r': 1.0 - ddd ** 0.2, 'x_w': 1.0 - ddd ** 0.9, 'x_k': 1.0 - ddd ** 0.7, 'x_v': 1.0 - ddd ** 0.7, 'x_a': 1.0 - ddd ** 0.9, 'x_g': 1.0 - ddd ** 0.2, 'W_r': w(ks[1]), 'W_w': w(ks[2]), 'W_k': w(ks[3]), 'W_v': w(ks[4]), 'W_a': w(ks[5]), 'W_g': w(ks[6]), 'W_out': jax.random.normal(ks[7], (D, D), jnp.float32) * s, 'b_out': jax.random.normal(ks[8], (D,), jnp.float32) * 0.01, 'gn_w': 1.0 + 0.1 * jax.random.normal(ks[9], (D,), jnp.float32), 'gn_b': 0.1 * jax.random.normal(ks[10], (D,), jnp.float32)}
    _L0_attn_in = _L0_attn_setup()

    def _L0_ffn_setup():
        import jax, jax.numpy as jnp
        import numpy as np
        HIDDEN = 512
        INTER = 2048
        key = jax.random.key(seed)
        k1, k2, k3, k4, k5 = jax.random.split(key, 5)
        hidden_states = jax.random.normal(k1, (4, 1024, HIDDEN), dtype=jnp.float32)
        W1 = jax.random.normal(k2, (HIDDEN, INTER), dtype=jnp.float32) * (1.0 / np.sqrt(HIDDEN))
        b1 = jax.random.normal(k3, (INTER,), dtype=jnp.float32) * 0.02
        W2 = jax.random.normal(k4, (INTER, HIDDEN), dtype=jnp.float32) * (1.0 / np.sqrt(INTER))
        b2 = jax.random.normal(k5, (HIDDEN,), dtype=jnp.float32) * 0.02
        return {'hidden_states': hidden_states, 'W1': W1, 'b1': b1, 'W2': W2, 'b2': b2}
    _L0_ffn_in = _L0_ffn_setup()
    _L0_c = _w((lambda *s: np.random.randn(*s).astype(np.float32) * 0.05)(2, 512))
    _L0_wmod = _w((lambda *s: np.random.randn(*s).astype(np.float32) * 0.05)(512, 6 * 512) * 512 ** (-0.5))
    _d = {'L0_attn_x': _L0_attn_in['x'], 'L0_attn_x_r': _L0_attn_in['x_r'], 'L0_attn_x_w': _L0_attn_in['x_w'], 'L0_attn_x_k': _L0_attn_in['x_k'], 'L0_attn_x_v': _L0_attn_in['x_v'], 'L0_attn_x_a': _L0_attn_in['x_a'], 'L0_attn_x_g': _L0_attn_in['x_g'], 'L0_attn_W_r': _L0_attn_in['W_r'], 'L0_attn_W_w': _L0_attn_in['W_w'], 'L0_attn_W_k': _L0_attn_in['W_k'], 'L0_attn_W_v': _L0_attn_in['W_v'], 'L0_attn_W_a': _L0_attn_in['W_a'], 'L0_attn_W_g': _L0_attn_in['W_g'], 'L0_attn_W_out': _L0_attn_in['W_out'], 'L0_attn_b_out': _L0_attn_in['b_out'], 'L0_attn_gn_w': _L0_attn_in['gn_w'], 'L0_attn_gn_b': _L0_attn_in['gn_b'], 'L0_ffn_W1': _L0_ffn_in['W1'], 'L0_ffn_b1': _L0_ffn_in['b1'], 'L0_ffn_W2': _L0_ffn_in['W2'], 'L0_ffn_b2': _L0_ffn_in['b2'], 'L0_c': _L0_c, 'L0_wmod': _L0_wmod}
    _x0 = _d['L0_attn_x']
    _d['L0_attn_x'] = jax.random.normal(jax.random.fold_in(jax.random.key(seed), 1), (2, 4096, 512), dtype=_x0.dtype)
    del _x0
    return _d

def reference(L0_attn_x, L0_attn_x_r, L0_attn_x_w, L0_attn_x_k, L0_attn_x_v, L0_attn_x_a, L0_attn_x_g, L0_attn_W_r, L0_attn_W_w, L0_attn_W_k, L0_attn_W_v, L0_attn_W_a, L0_attn_W_g, L0_attn_W_out, L0_attn_b_out, L0_attn_gn_w, L0_attn_gn_b, L0_ffn_W1, L0_ffn_b1, L0_ffn_W2, L0_ffn_b2, L0_c, L0_wmod):

    def _L0_attn_ref(x, x_r, x_w, x_k, x_v, x_a, x_g, W_r, W_w, W_k, W_v, W_a, W_g, W_out, b_out, gn_w, gn_b):
        import jax, jax.numpy as jnp
        import numpy as np
        B, N, D, H = (4, 2048, 512, 16)
        GN_EPS = 0.00064
        b, n, d = x.shape
        prev = jnp.concatenate([jnp.zeros_like(x[:, :1]), x[:, :-1]], axis=1)
        xx = prev - x
        lin = lambda mix, W: (x + xx * mix) @ W.T
        r = jax.nn.sigmoid(lin(x_r, W_r))
        decay = jnp.exp(-jax.nn.softplus(lin(x_w, W_w)))
        k = jnp.tanh(lin(x_k, W_k))
        v = lin(x_v, W_v)
        alpha = jax.nn.sigmoid(lin(x_a, W_a))
        g = jax.nn.sigmoid(lin(x_g, W_g))
        u = alpha * k * v

        def step(state, inp):
            d_t, u_t, r_t = inp
            state = state * d_t + u_t
            return (state, r_t * state)
        inputs_tm = (jnp.swapaxes(decay, 0, 1), jnp.swapaxes(u, 0, 1), jnp.swapaxes(r, 0, 1))
        state0 = jnp.zeros((b, d), x.dtype)
        _, mixed_tm = jax.lax.scan(step, state0, inputs_tm)
        mixed = jnp.swapaxes(mixed_tm, 0, 1)
        m = mixed.reshape(b * n, H, d // H)
        mu = m.mean(-1, keepdims=True)
        var = ((m - mu) ** 2).mean(-1, keepdims=True)
        mn = ((m - mu) / jnp.sqrt(var + GN_EPS)).reshape(b, n, d)
        mn = mn * gn_w + gn_b
        return mn * g @ W_out.T + b_out

    def _L0_ffn_ref(hidden_states, W1, b1, W2, b2):
        import jax, jax.numpy as jnp
        import numpy as np
        HIDDEN = 512
        INTER = 2048
        h = jax.nn.relu(jnp.einsum('bsh,hi->bsi', hidden_states, W1) + b1)
        return jnp.einsum('bsi,ih->bsh', h, W2) + b2
    x = L0_attn_x
    mod = (_silu(L0_c) @ L0_wmod).reshape(L0_c.shape[0], 6, 1, -1)
    sa, ca, ga, sb, cb, gb = (mod[:, 0], mod[:, 1], mod[:, 2], mod[:, 3], mod[:, 4], mod[:, 5])
    ga = (2 * (ga >= 0) - 1) * jnp.maximum(jnp.abs(ga), 0.25)
    gb = (2 * (gb >= 0) - 1) * jnp.maximum(jnp.abs(gb), 0.25)
    h = _layernorm(x, axis=-1) * (1 + ca) + sa
    x = x + ga * _L0_attn_ref(h, L0_attn_x_r, L0_attn_x_w, L0_attn_x_k, L0_attn_x_v, L0_attn_x_a, L0_attn_x_g, L0_attn_W_r, L0_attn_W_w, L0_attn_W_k, L0_attn_W_v, L0_attn_W_a, L0_attn_W_g, L0_attn_W_out, L0_attn_b_out, L0_attn_gn_w, L0_attn_gn_b)
    h = _layernorm(x, axis=-1) * (1 + cb) + sb
    x = x + gb * _L0_ffn_ref(h, L0_ffn_W1, L0_ffn_b1, L0_ffn_W2, L0_ffn_b2)
    return x

_drawn_inputs = setup_inputs


def setup_inputs(seed=0):
    import zlib

    import numpy as np

    out = dict(_drawn_inputs(seed))
    spreads = {}
    factors = {'L0_attn_x_r': 4.806,
     'L0_attn_x_w': 4.149,
     'L0_attn_x_g': 4.605,
     'L0_attn_b_out': 27.675,
     'L0_attn_gn_w': 4.397,
     'L0_attn_gn_b': 4.175,
     'L0_ffn_b1': 8.0,
     'L0_ffn_b2': 8.0}
    for name, (base, spread) in spreads.items():
        noise = np.random.default_rng([zlib.crc32(name.encode()), seed]).standard_normal(out[name].shape)
        drawn = base * np.exp(spread * noise) if base else spread * noise
        out[name] = jnp.asarray(drawn.astype(out[name].dtype))
    for name, factor in factors.items():
        out[name] = (out[name] * factor).astype(out[name].dtype)
    return out
```

```python
from contextlib import ExitStack

import concourse.bass as bass
from concourse import mybir
from concourse.alu_op_type import AluOpType as ALU

F32 = mybir.dt.float32
F32R = mybir.dt.float32r
ACT = mybir.ActivationFunctionType

P = 128
D = 512
KC = D // P
TOK = 512
SUB = TOK // P
HEADS = 16
GROUP = D // HEADS
GPC = P // GROUP
INTER = 2048
JC = INTER // P
LN_EPS = 1e-5
GN_EPS = 0.00064
GATE_MIN = 0.25

PROJ = ["k", "a", "v", "w", "r", "g"]
NP = len(PROJ)
PIECES = NP * KC
HI_RING = 4
F32_RING = 3
GATE_RING = 3
PROJ_BANKS = 6
AUX = [6, 7]
STEPS = 2 * KC - 1
STAGES = 6


def wait(engine, semaphore, value):
    if not isinstance(value, int) or value > 0:
        engine.wait_ge(semaphore, value)


def split_product(pe, acc, a_hi, a_lo, b_hi, b_lo, first, last):
    pe.matmul(acc, a_hi, b_hi, start=first, stop=False)
    pe.matmul(acc, a_hi, b_lo, start=False, stop=False)
    return pe.matmul(acc, a_lo, b_hi, start=False, stop=last)


def moments_steps(dve, step, steps_before, stats, mean, var_eps, scratch):
    mean_e, mean_o, m2_e, m2_o = (stats[:, :, q] for q in (1, 4, 2, 5))
    diff, m2 = scratch[:, 0, :], scratch[:, 1, :]
    dve.tensor_tensor(diff, mean_e, mean_o, ALU.subtract).then_inc(step, 1)
    dve.scalar_tensor_tensor(m2, m2_e, D * LN_EPS, m2_o, ALU.add, ALU.add).then_inc(step, 1)
    dve.tensor_tensor(mean, mean_e, mean_o, ALU.add).then_inc(step, 1)
    dve.wait_ge(step, steps_before + 3)
    dve.scalar_tensor_tensor(diff, diff, 0.25, diff, ALU.mult, ALU.mult).then_inc(step, 1)
    dve.tensor_scalar(mean, mean, 0.5, None, ALU.mult).then_inc(step, 1)
    dve.wait_ge(step, steps_before + 5)
    dve.scalar_tensor_tensor(var_eps, m2, 1.0 / D, diff, ALU.mult, ALU.add).then_inc(step, 1)


MOMENT_STEPS = 6


def setup_block(nc, tag, wmod, silu_in, bias_row, shift_q, scale_q, gate_q, batches,
                shift, scale, gate, bias, weights):
    wmod_view = wmod.rearrange("(k p) n -> p k n", p=P)
    loads = [wmod_view[:, :, q * D:(q + 1) * D] for q in (scale_q, shift_q, gate_q)]
    n_mod = len(loads)
    loads += [source for source, _, _ in weights]
    with ExitStack() as ctx:
        def sb(name, shape, dt=F32):
            return ctx.enter_context(nc.sbuf_tensor(f"{tag}_{name}", shape, dt))

        def sem(name):
            return ctx.enter_context(nc.semaphore(f"{tag}_{name}"))

        stage = sb("stage", [P, STAGES, KC, D])
        cT = sb("cT", [P, KC, batches])
        sig = sb("sig", [P, KC, batches])
        silu = sb("silu", [P, KC, batches])
        raw = sb("raw", [P, batches, D])
        sign = sb("sign", [P, batches, D])
        size = sb("size", [P, batches, D])
        columns = ctx.enter_context(nc.psum_tensor(f"{tag}_columns", [P, 512], F32))
        rows = ctx.enter_context(nc.psum_tensor(f"{tag}_rows", [P, batches, 512], F32))

        c_in = sem("c_in")
        bias_in = sem("bias_in")
        stage_in = [sem(f"stage_in{s}") for s in range(STAGES)]
        sig_ready = sem("sig_ready")
        silu_ready = sem("silu_ready")
        mod_done = sem("mod_done")
        hi_done = sem("hi_done")
        lo_dve = sem("lo_dve")
        lo_pool = sem("lo_pool")
        chain = sem("chain")

        def taken_by_pool(n):
            return n % 3 == 2

        def stage_free(engine, n):
            old = n - STAGES
            if old < 0:
                return
            if old < n_mod:
                engine.wait_ge(mod_done, old + 1)
                return
            old -= n_mod
            if taken_by_pool(old):
                engine.wait_ge(lo_pool, sum(taken_by_pool(m) for m in range(old + 1)))
            else:
                engine.wait_ge(lo_dve, sum(not taken_by_pool(m) for m in range(old + 1)))

        def arrived(engine, n):
            engine.wait_ge(stage_in[n % STAGES], 16 * (n // STAGES + 1))

        with nc.Block() as block:
            @block.sync
            def _(sp):
                sp.dma_start(cT[:], silu_in).then_inc(c_in, 16)
                sp.dma_start(bias, bias_row.partition_broadcast(P)).then_inc(bias_in, 16)
                for n, source in enumerate(loads):
                    stage_free(sp, n)
                    sp.dma_start(stage[:, n % STAGES], source).then_inc(stage_in[n % STAGES], 16)
                sp.wait_ge(bias_in, 16)

            @block.scalar
            def _(act):
                act.wait_ge(c_in, 16)
                act.activation(sig[:], cT[:], ACT.Sigmoid).then_inc(sig_ready, 1)
                for n, (_, hi, _) in enumerate(weights):
                    arrived(act, n_mod + n)
                    act.activation(hi, stage[:, (n_mod + n) % STAGES], ACT.Copy).then_inc(hi_done, 1)

            @block.tensor
            def _(pe):
                pe.wait_ge(silu_ready, 1)
                for n in range(2):
                    arrived(pe, n)
                    for c in range(KC):
                        at = (n * KC + c) * batches
                        for k in range(KC):
                            last = pe.matmul(columns[:, at:at + batches],
                                             stage[:, n, k, c * P:(c + 1) * P], silu[:, k, :],
                                             start=k == 0, stop=k == KC - 1)
                    last.then_inc(mod_done, 1)
                arrived(pe, 2)
                for b in range(batches):
                    for k in range(KC):
                        last = pe.matmul(rows[:, b, :], silu[:, k, b:b + 1].broadcast_to([P, P]),
                                         stage[:, 2, k, :], start=k == 0, stop=k == KC - 1)
                last.then_inc(mod_done, 1)

            @block.vector
            def _(dve):
                dve.wait_ge(sig_ready, 1)
                dve.tensor_tensor(silu[:], cT[:], sig[:], ALU.mult).then_inc(silu_ready, 1)
                dve.wait_ge(mod_done, 3)
                got = columns[:, 0:2 * KC * batches].rearrange("p (n c b) -> p n b c", n=2, c=KC)
                for b in range(batches):
                    dve.tensor_scalar(scale[:, b, :], got[:, 0, b, :], 1.0, None, ALU.add)
                    dve.tensor_copy(shift[:, b, :], got[:, 1, b, :])
                dve.tensor_scalar(raw[:], rows[:], 2.0, None, ALU.mult).then_inc(chain, 1)
                dve.wait_ge(chain, 1)
                dve.tensor_scalar(sign[:], raw[:], 0.0, 0.5, ALU.is_ge, ALU.subtract)\
                   .then_inc(chain, 1)
                dve.scalar_tensor_tensor(size[:], raw[:], -1.0, raw[:], ALU.mult, ALU.max)\
                   .then_inc(chain, 1)
                dve.wait_ge(chain, 3)
                dve.scalar_tensor_tensor(gate, size[:], 2 * GATE_MIN, sign[:], ALU.max, ALU.mult)
                for n, (_, hi, lo) in enumerate(weights):
                    if not taken_by_pool(n):
                        dve.wait_ge(hi_done, n + 1)
                        dve.tensor_tensor(lo, stage[:, (n_mod + n) % STAGES], hi.bitcast(F32),
                                          ALU.subtract).then_inc(lo_dve, 1)

            @block.gpsimd
            def _(pool):
                for n, (_, hi, lo) in enumerate(weights):
                    if taken_by_pool(n):
                        pool.wait_ge(hi_done, n + 1)
                        pool.tensor_tensor(lo, stage[:, (n_mod + n) % STAGES], hi.bitcast(F32),
                                           ALU.subtract).then_inc(lo_pool, 1)


def attention(nc, x, x2, mixes, w_proj, w_out, b_out, gn, cT, wmod, identity, centering,
              group_mean, keep_in, batches, seq):
    tokens = x.shape[0]
    blocks = tokens // TOK
    per_batch = seq // TOK
    x_view = x.rearrange("(n p) d -> n p d", p=P)
    x2_view = x2.rearrange("(n p) d -> n p d", p=P)

    with ExitStack() as ctx:
        def sb(name, shape, dt=F32):
            return ctx.enter_context(nc.sbuf_tensor(name, shape, dt))

        def sem(name):
            return ctx.enter_context(nc.semaphore(name))

        w_hi = sb("w_hi", [P, NP + 1, KC, D], F32R)
        w_lo = sb("w_lo", [P, NP + 1, KC, D], F32R)
        modulation = sb("modulation", [P, batches, 2, KC])
        gate = sb("gate", [P, batches, D])
        bias = sb("bias", [P, D])

        views = [w.rearrange("(k p) n -> p k n", p=P) for w in (*w_proj, w_out)]
        setup_block(nc, "sa", wmod, cT, b_out, 0, 1, 2, batches, modulation[:, :, 0, :],
                    modulation[:, :, 1, :], gate[:],
                    bias[:], [(v, w_hi[:, m], w_lo[:, m]) for m, v in enumerate(views)])

        ident = sb("ident", [P, P])
        center = sb("center", [P, P])
        g_mean = sb("g_mean", [P, GPC])
        mix = sb("mix", [P, PIECES])
        unmix = sb("unmix", [P, PIECES])
        gn_wb = sb("gn_wb", [P, 2, KC])
        keep = sb("keep", [P, blocks + 1])
        current = sb("current", [P, 2, KC])
        keep_now = sb("keep_now", [P, 1])
        half = sb("half", [P, SUB * HEADS])
        state = sb("state", [P, KC])

        xt = sb("xt", [P, SUB, D])
        stats = sb("stats", [P, SUB, 6])
        mean = sb("mean", [P, SUB])
        scratch = sb("scratch", [P, 2, SUB])
        var_eps = sb("var_eps", [P, SUB])
        rstd = sb("rstd", [P, SUB])
        hT = sb("hT", [P, KC, 1 + TOK])
        mixed_in = sb("mixed_in", [P, F32_RING, TOK])
        in_hi = sb("in_hi", [P, HI_RING, TOK], F32R)
        in_lo = sb("in_lo", [P, HI_RING, TOK], F32R)
        u = sb("u", [P, KC, TOK])
        gates = sb("gates", [P, GATE_RING, TOK])
        g_sig = sb("g_sig", [P, KC, TOK])
        square = rstd_wide = scaled = sb("square_wide_scaled", [P, 2, TOK])
        g_var = sb("g_var", [P, SUB * HEADS])
        g_rstd = sb("g_rstd", [P, SUB * HEADS])
        y_hi = sb("y_hi", [P, KC, TOK], F32R)
        y_lo = sb("y_lo", [P, KC, TOK], F32R)
        res = sb("res", [P, 2, D])
        ps = ctx.enter_context(nc.psum_tensor("ps", [P, 8, 512], F32))

        const_in = sem("const_in")
        const_set = sem("const_set")
        unmix_set = sem("unmix_set")
        x_in = sem("x_in")
        ln_stats = sem("ln_stats")
        ln_step = sem("ln_step")
        ln_rstd = sem("ln_rstd")
        xn_ready = sem("xn_ready")
        t_done = sem("t_done")
        h_ready = sem("h_ready")
        carried = sem("carried")
        prev_scaled = sem("prev_scaled")
        mix_ready = sem("mix_ready")
        hi_ready = sem("hi_ready")
        lo_ready = sem("lo_ready")
        proj_step = sem("proj_step")
        act_out = sem("act_out")
        v_out = sem("v_out")
        gate_used = sem("gate_used")
        state_kept = sem("state_kept")
        center_done = sem("center_done")
        centered = sem("centered")
        squared = sem("squared")
        var_done = sem("var_done")
        g_var_set = sem("g_var_set")
        g_rstd_set = sem("g_rstd_set")
        wide_set = sem("wide_set")
        wide_done = sem("wide_done")
        normed = sem("normed")
        affine = sem("affine")
        gated = sem("gated")
        y_hi_set = sem("y_hi_set")
        y_lo_set = sem("y_lo_set")
        out_done = sem("out_done")
        out_biased = sem("out_biased")
        out_scaled = sem("out_scaled")
        res_in = [sem(f"res_in{s}") for s in range(2)]
        x2_ready = sem("x2_ready")
        x2_out = [sem(f"x2_out{s}") for s in range(2)]

        def aux(n):
            return ps[:, AUX[n % 2]]

        def proj_bank(n):
            return ps[:, n % PROJ_BANKS]

        def input_used(i, n):
            if n < 0:
                n, i = n + PIECES, i - 1
            m, k = divmod(n, KC)
            return STEPS * NP * i + STEPS * m + (k + 1 if k < KC - 1 else STEPS)

        def output_done(i, m, o):
            return STEPS * NP * i + STEPS * m + KC + o

        block = ctx.enter_context(nc.Block())

        @block.sync
        def _(sp):
            loads = [(ident, identity), (center, centering), (g_mean, group_mean),
                     (mix, mixes), (gn_wb, gn), (keep, keep_in)]
            for tile, source in loads:
                sp.dma_start(tile[:], source).then_inc(const_in, 16)

            def load_x(b):
                wait(sp, t_done, SUB * b)
                sp.dma_start(xt[:], x_view[bass.ds(SUB * b, SUB)].rearrange("s p d -> p s d"))\
                  .then_inc(x_in, 16)

            def residual(j):
                def load(s):
                    if s >= 2:
                        sp.wait_ge(x2_out[s % 2], 16 * (2 * j + 1))
                    sp.dma_start(res[:, s % 2], x_view[SUB * j + s]).then_inc(res_in[s % 2], 16)

                def store(s):
                    sp.wait_ge(x2_ready, SUB * j + s + 1)
                    sp.dma_start(x2_view[SUB * j + s], res[:, s % 2]).then_inc(x2_out[s % 2], 16)

                load(0)
                load(1)
                for s in range(2, SUB):
                    store(s - 2)
                    load(s)
                store(SUB - 2)
                store(SUB - 1)

            def both_stored(j):
                for s in range(2):
                    sp.wait_ge(x2_out[s], 16 * 2 * (j + 1))

            def body(i, before, after):
                if before:
                    residual(i - 1)
                    both_stored(i - 1)
                if after:
                    load_x(i + 1)

            load_x(0)
            body(0, False, True)
            with sp.Fori(1, blocks - 1) as i:
                body(i, True, True)
            body(blocks - 1, True, False)
            residual(blocks - 1)
            both_stored(blocks - 1)

        @block.tensor
        def _(pe):
            def bank_free(i, n):
                n -= PROJ_BANKS
                if n < 0:
                    n, i = n + PIECES, i - 1
                m, o = divmod(n, KC)
                if PROJ[m] == "v":
                    wait(pe, v_out, KC * i + o + 1)
                else:
                    wait(pe, act_out, (PIECES - KC) * i + n + 1 - (KC if m > 2 else 0))

            def project(i, m, k):
                n = m * KC + k
                slot = n % HI_RING
                pe.wait_ge(lo_ready, PIECES * i + n + 1)
                for o in range(KC):
                    if k == 0:
                        bank_free(i, m * KC + o)
                    cols = slice(o * P, (o + 1) * P)
                    last = split_product(pe, proj_bank(m * KC + o), w_hi[:, m, k, cols],
                                         w_lo[:, m, k, cols], in_hi[:, slot], in_lo[:, slot],
                                         k == 0, k == KC - 1)
                    if k == KC - 1 or o == KC - 1:
                        last.then_inc(proj_step, 1)

            def transpose_x(b):
                for s in range(SUB):
                    pe.wait_ge(xn_ready, SUB * b + s + 1)
                    if s < 2 and isinstance(b, int) and b < 2:
                        wait(pe, h_ready, SUB * (b - 1) + s + 3)
                    elif s < 2:
                        pe.wait_ge(out_biased, SUB * (b - 2) + s + 3)
                    else:
                        pe.wait_ge(h_ready, SUB * b + s - 1)
                    for c in range(KC):
                        last = pe.transpose(aux(s + 1)[:, c * P:(c + 1) * P],
                                            xt[:, s, c * P:(c + 1) * P], ident[:])
                    last.then_inc(t_done, 1)

            def center_chunk(i, c, after):
                pe.wait_ge(gate_used, 3 * KC * i + 2 * KC + c + 1)
                if c >= 2:
                    pe.wait_ge(centered, KC * i + c - 1)
                elif after:
                    pe.wait_ge(h_ready, SUB * (i + 1) + c + 3)
                else:
                    pe.wait_ge(out_biased, SUB * (i - 1) + c + 3)
                pe.matmul(aux(c + 1), center[:], u[:, c, :], start=True, stop=True)\
                  .then_inc(center_done, 1)

            def variance(i, c):
                pe.wait_ge(squared, KC * i + c + 1)
                if c == 0:
                    pe.wait_ge(centered, KC * i + KC)
                for s in range(SUB):
                    at = s * HEADS + c * GPC
                    last = pe.matmul(aux(0)[:, at:at + GPC], square[:, c % 2, s * P:(s + 1) * P],
                                     g_mean[:], start=True, stop=True)
                last.then_inc(var_done, 1)

            def widen(j, s):
                pe.wait_ge(wide_set, SUB * j + s + 1)
                if s == 1:
                    pe.wait_ge(g_var_set, j + 1)
                if s >= 2:
                    pe.wait_ge(normed, SUB * j + s - 1)
                for c in range(KC):
                    last = pe.transpose(aux(s + 1)[:, c * P:(c + 1) * P],
                                        rstd_wide[:, s % 2, c * P:(c + 1) * P], ident[:])
                last.then_inc(wide_done, 1)

            def output(j):
                pe.wait_ge(y_lo_set, KC * (j + 1))
                for s in range(SUB):
                    if s < 2:
                        pe.wait_ge(normed, SUB * j + s + 3)
                    else:
                        pe.wait_ge(out_biased, SUB * j + s - 1)
                    for k in range(KC):
                        rows = slice(s * P, (s + 1) * P)
                        last = split_product(pe, aux(s + 1), y_hi[:, k, rows], y_lo[:, k, rows],
                                             w_hi[:, NP, k, :], w_lo[:, NP, k, :],
                                             k == 0, k == KC - 1)
                    last.then_inc(out_done, 1)

            def body(i, before, after):
                for k in range(KC):
                    project(i, 0, k)
                    if before and k in (1, 2):
                        widen(i - 1, 2 * k - 2)
                        widen(i - 1, 2 * k - 1)
                for k in range(KC):
                    project(i, 1, k)
                if before:
                    output(i - 1)
                for m in (2, 3, 4):
                    for k in range(KC):
                        project(i, m, k)
                if after:
                    transpose_x(i + 1)
                for k in range(KC):
                    project(i, 5, k)
                    if k < 2:
                        center_chunk(i, 2 * k, after)
                        center_chunk(i, 2 * k + 1, after)
                    else:
                        variance(i, 2 * k - 4)
                        variance(i, 2 * k - 3)

            pe.wait_ge(const_in, 6 * 16)
            transpose_x(0)
            body(0, False, True)
            with pe.Fori(1, blocks - 1) as i:
                body(i, True, True)
            body(blocks - 1, True, False)
            for s in range(SUB):
                widen(blocks - 1, s)
            output(blocks - 1)

        @block.scalar
        def _(act):
            def scale_prev(b, m, c):
                n = m * KC + c
                if n == 0:
                    act.wait_ge(h_ready, SUB * (b + 1))
                    wait(act, carried, b)
                wait(act, lo_ready, PIECES * b + n + 1 - F32_RING)
                act.activation(mixed_in[:, n % F32_RING], hT[:, c, 0:TOK], ACT.Copy,
                               scale=mix[:, n:n + 1]).then_inc(prev_scaled, 1)

            def out_of_psum(i, m):
                name = PROJ[m]
                func = ACT.Tanh if name == "k" else ACT.Sigmoid
                for o in range(KC):
                    if name == "k":
                        wait(act, y_lo_set, KC * (i - 1) + o + 1)
                        target = u[:, o, :]
                    elif name == "g":
                        wait(act, gated, KC * (i - 1) + o + 1)
                        target = g_sig[:, o, :]
                    else:
                        n = {"a": 0, "w": 1, "r": 2}[name] * KC + o
                        wait(act, gate_used, 3 * KC * i + n + 1 - GATE_RING)
                        target = gates[:, n % GATE_RING]
                    act.wait_ge(proj_step, output_done(i, m, o))
                    act.activation(target, proj_bank(m * KC + o), func,
                                   scale=-1.0 if name == "w" else 1.0).then_inc(act_out, 1)

            def modulated(b):
                wait(act, mix_ready, PIECES * b)
                if not (isinstance(b, int) and b == 0):
                    act.activation(hT[:, :, 0:1], hT[:, :, TOK:TOK + 1], ACT.Copy,
                                   scale=keep_now[:]).then_inc(carried, 1)
                for s in range(SUB):
                    act.wait_ge(t_done, SUB * b + s + 1)
                    if s == SUB - 1:
                        wait(act, carried, b)
                    for c in range(KC):
                        last = act.activation(
                            hT[:, c, 1 + s * P:1 + (s + 1) * P], aux(s + 1)[:, c * P:(c + 1) * P],
                            ACT.Identity, bias=current[:, 0, c:c + 1],
                            scale=current[:, 1, c:c + 1])
                    last.then_inc(h_ready, 1)

            def group_affine(j):
                for c in range(KC):
                    act.wait_ge(normed, SUB * (j + 1))
                    act.activation(u[:, c, :], u[:, c, :], ACT.Identity, bias=gn_wb[:, 1, c:c + 1],
                                   scale=gn_wb[:, 0, c:c + 1]).then_inc(affine, 1)

            def center_out(i, c):
                act.wait_ge(center_done, KC * i + c + 1)
                act.activation(u[:, c, :], aux(c + 1), ACT.Copy).then_inc(centered, 1)

            def body(i, before, after):
                for c in range(KC):
                    scale_prev(i, 1, c)
                if before:
                    group_affine(i - 1)
                out_of_psum(i, 0)
                for m in range(1, NP - 1):
                    for c in range(KC):
                        scale_prev(i, m + 1, c)
                    if PROJ[m] != "v":
                        out_of_psum(i, m)
                if after:
                    modulated(i + 1)
                for c in range(KC):
                    if after:
                        scale_prev(i + 1, 0, c)
                    center_out(i, c)
                out_of_psum(i, NP - 1)

            act.wait_ge(const_in, 6 * 16)
            act.wait_ge(const_set, 3)
            modulated(0)
            for c in range(KC):
                scale_prev(0, 0, c)
            body(0, False, True)
            with act.Fori(1, blocks - 1) as i:
                body(i, True, True)
            body(blocks - 1, True, False)
            group_affine(blocks - 1)

        @block.vector
        def _(dve):
            def layer_norm(b):
                dve.tensor_scalar(current[:], modulation[:, b // per_batch], 1.0, None, ALU.mult)
                dve.tensor_scalar(keep_now[:], keep[:, bass.ds(b, 1)], 1.0, None, ALU.mult)
                dve.wait_ge(x_in, 16 * (b + 1))
                for s in range(SUB):
                    dve.bn_stats(stats[:, s, :], xt[:, s, :]).then_inc(ln_stats, 1)
                dve.wait_ge(ln_stats, SUB * (b + 1))
                moments_steps(dve, ln_step, MOMENT_STEPS * b, stats, mean[:], var_eps[:], scratch)
                dve.wait_ge(ln_rstd, b + 1)
                for s in range(SUB):
                    dve.tensor_scalar(xt[:, s, :], xt[:, s, :], mean[:, s:s + 1],
                                      rstd[:, s:s + 1], ALU.subtract, ALU.mult)\
                       .then_inc(xn_ready, 1)

            def mix_piece(b, m, c):
                n = m * KC + c
                made = mixed_in[:, n % F32_RING]
                dve.wait_ge(prev_scaled, PIECES * b + n + 1)
                dve.scalar_tensor_tensor(made, hT[:, c, 1:1 + TOK], unmix[:, n:n + 1], made,
                                         ALU.mult, ALU.add).then_inc(mix_ready, 1)
                dve.wait_ge(mix_ready, PIECES * b + n + 1)
                wait(dve, proj_step, input_used(b, n - HI_RING) if n >= HI_RING or
                     not isinstance(b, int) or b > 0 else 0)
                dve.tensor_copy(in_hi[:, n % HI_RING], made).then_inc(hi_ready, 1)

            def use_a(i, c):
                dve.wait_ge(act_out, 5 * KC * i + KC + c + 1)
                dve.tensor_tensor(u[:, c, :], u[:, c, :], gates[:, c % GATE_RING], ALU.mult)\
                   .then_inc(gate_used, 1)

            def use_v(i, c):
                dve.wait_ge(proj_step, output_done(i, 2, c))
                dve.wait_ge(gate_used, 3 * KC * i + c + 1)
                dve.tensor_tensor(u[:, c, :], u[:, c, :], proj_bank(2 * KC + c), ALU.mult)\
                   .then_inc(v_out, 1)

            def scan(i, c):
                dve.wait_ge(act_out, 5 * KC * i + 2 * KC + c + 1)
                dve.wait_ge(v_out, KC * i + c + 1)
                wait(dve, state_kept, KC * (i - 1) + c + 1)
                dve.tensor_tensor_scan(u[:, c, :], gates[:, (KC + c) % GATE_RING], u[:, c, :],
                                       state[:, c:c + 1], ALU.mult, ALU.add)\
                   .then_inc(gate_used, 1)

            def keep_state(i, c):
                dve.wait_ge(gate_used, 3 * KC * i + KC + c + 1)
                dve.tensor_scalar(state[:, c:c + 1], u[:, c, TOK - 1:TOK],
                                  keep[:, bass.ds(i + 1, 1)], None, ALU.mult)\
                   .then_inc(state_kept, 1)

            def use_r(i, c):
                dve.wait_ge(act_out, 5 * KC * i + 3 * KC + c + 1)
                dve.wait_ge(state_kept, KC * i + c + 1)
                dve.tensor_tensor(u[:, c, :], u[:, c, :], gates[:, (2 * KC + c) % GATE_RING],
                                  ALU.mult).then_inc(gate_used, 1)

            def group_variance(j):
                dve.wait_ge(var_done, KC * (j + 1))
                dve.tensor_scalar(g_var[:], aux(0)[:, 0:SUB * HEADS], GN_EPS, None, ALU.add)\
                   .then_inc(g_var_set, 1)

            def wide(j, s):
                dve.wait_ge(g_rstd_set, j + 1)
                if s >= 2:
                    dve.wait_ge(wide_done, SUB * j + s - 1)
                dve.tensor_copy(
                    rstd_wide[:, s % 2].rearrange("p (g c) -> p g c", c=GROUP),
                    g_rstd[:, s * HEADS:(s + 1) * HEADS].unsqueeze(2)
                    .broadcast_to([P, HEADS, GROUP])).then_inc(wide_set, 1)

            def normalise(j, s):
                dve.wait_ge(wide_done, SUB * j + s + 1)
                part = u[:, :, s * P:(s + 1) * P]
                dve.tensor_tensor(part, part, aux(s + 1).rearrange("p (c t) -> p c t", c=KC),
                                  ALU.mult).then_inc(normed, 1)

            def gate_y(j, c):
                dve.wait_ge(affine, KC * j + c + 1)
                dve.tensor_tensor(u[:, c, :], u[:, c, :], g_sig[:, c, :], ALU.mult)\
                   .then_inc(gated, 1)
                dve.wait_ge(gated, KC * j + c + 1)
                dve.tensor_copy(y_hi[:, c, :], u[:, c, :]).then_inc(y_hi_set, 1)

            def scale_output(j, s):
                slot = scaled[:, s % 2]
                dve.wait_ge(out_done, SUB * j + s + 1)
                if s >= 2:
                    dve.wait_ge(x2_ready, SUB * j + s - 1)
                dve.tensor_tensor(slot, aux(s + 1), bias[:], ALU.add).then_inc(out_biased, 1)
                dve.wait_ge(out_biased, SUB * j + s + 1)
                dve.tensor_tensor(slot, slot, gate[:, j // per_batch, :], ALU.mult)\
                   .then_inc(out_scaled, 1)

            def body(i, before, after):
                j = i - 1
                if before:
                    group_variance(j)
                    wide(j, 0)
                    wide(j, 1)
                mix_piece(i, 1, 0)
                mix_piece(i, 1, 1)
                if before:
                    normalise(j, 0)
                    wide(j, 2)
                    normalise(j, 1)
                    wide(j, 3)
                mix_piece(i, 1, 2)
                if before:
                    normalise(j, 2)
                    normalise(j, 3)
                    for c in range(KC):
                        gate_y(j, c)
                mix_piece(i, 1, 3)
                for c in range(KC):
                    mix_piece(i, 2, c)
                for c in range(KC):
                    use_a(i, c)
                if before:
                    for s in range(SUB):
                        scale_output(j, s)
                for c in range(KC):
                    mix_piece(i, 3, c)
                for c in range(KC):
                    use_v(i, c)
                for c in range(KC):
                    mix_piece(i, 4, c)
                for c in range(KC):
                    scan(i, c)
                    keep_state(i, c)
                if after:
                    layer_norm(i + 1)
                for c in range(KC):
                    mix_piece(i, 5, c)
                for c in range(KC):
                    use_r(i, c)
                if after:
                    for c in range(KC):
                        mix_piece(i + 1, 0, c)

            dve.wait_ge(const_in, 6 * 16)
            dve.wait_ge(const_set, 3)
            dve.tensor_scalar(unmix[:], mix[:], -1.0, 1.0, ALU.mult, ALU.add).then_inc(unmix_set, 1)
            dve.wait_ge(unmix_set, 1)
            layer_norm(0)
            for c in range(KC):
                mix_piece(0, 0, c)
            body(0, False, True)
            with dve.Fori(1, blocks - 1) as i:
                body(i, True, True)
            body(blocks - 1, True, False)
            group_variance(blocks - 1)
            for s in range(SUB):
                wide(blocks - 1, s)
                normalise(blocks - 1, s)
            for c in range(KC):
                gate_y(blocks - 1, c)
            for s in range(SUB):
                scale_output(blocks - 1, s)

        @block.gpsimd
        def _(pool):
            def lo_piece(b, m, c):
                n = m * KC + c
                pool.wait_ge(hi_ready, PIECES * b + n + 1)
                pool.tensor_tensor(in_lo[:, n % HI_RING], mixed_in[:, n % F32_RING],
                                   in_hi[:, n % HI_RING].bitcast(F32), ALU.subtract)\
                    .then_inc(lo_ready, 1)

            def layer_norm_rstd(b):
                pool.wait_ge(ln_step, MOMENT_STEPS * (b + 1))
                pool.tensor_tensor(rstd[:], var_eps[:], half[:, 0:SUB], ALU.pow)\
                    .then_inc(ln_rstd, 1)

            def group_rstd(j):
                pool.wait_ge(g_var_set, j + 1)
                pool.tensor_tensor(g_rstd[:], g_var[:], half[:], ALU.pow)\
                    .then_inc(g_rstd_set, 1)

            def square_chunk(i, c):
                pool.wait_ge(centered, KC * i + c + 1)
                wait(pool, var_done, KC * i + c - 1)
                pool.tensor_tensor(square[:, c % 2], u[:, c, :], u[:, c, :], ALU.mult)\
                    .then_inc(squared, 1)

            def y_lo_chunk(j, c):
                pool.wait_ge(y_hi_set, KC * j + c + 1)
                pool.tensor_tensor(y_lo[:, c, :], u[:, c, :], y_hi[:, c, :].bitcast(F32),
                                   ALU.subtract).then_inc(y_lo_set, 1)

            def residual(j, s):
                pool.wait_ge(out_scaled, SUB * j + s + 1)
                pool.wait_ge(res_in[s % 2], 16 * (2 * j + s // 2 + 1))
                pool.tensor_tensor(res[:, s % 2], scaled[:, s % 2], res[:, s % 2], ALU.add)\
                    .then_inc(x2_ready, 1)

            def body(i, before, after):
                if before:
                    group_rstd(i - 1)
                for c in range(KC - 1):
                    lo_piece(i, 1, c)
                if before:
                    for c in range(KC):
                        y_lo_chunk(i - 1, c)
                lo_piece(i, 1, KC - 1)
                for c in range(KC):
                    lo_piece(i, 2, c)
                if before:
                    for s in range(SUB):
                        residual(i - 1, s)
                for m in (3, 4):
                    for c in range(KC):
                        lo_piece(i, m, c)
                if after:
                    layer_norm_rstd(i + 1)
                for c in range(KC):
                    lo_piece(i, 5, c)
                for c in range(KC):
                    if after:
                        lo_piece(i + 1, 0, c)
                    square_chunk(i, c)

            pool.memset(half[:], -0.5).then_inc(const_set, 1)
            pool.memset(state[:], 0.0).then_inc(const_set, 1)
            pool.memset(hT[:, :, 0:1], 0.0).then_inc(const_set, 1)
            pool.wait_ge(const_set, 3)
            layer_norm_rstd(0)
            for c in range(KC):
                lo_piece(0, 0, c)
            body(0, False, True)
            with pool.Fori(1, blocks - 1) as i:
                body(i, True, True)
            body(blocks - 1, True, False)
            group_rstd(blocks - 1)
            for c in range(KC):
                y_lo_chunk(blocks - 1, c)
            for s in range(SUB):
                residual(blocks - 1, s)


def feed_forward(nc, x2, out, w1, w2, b1_in, b2, cT, wmod, identity, batches, seq):
    tokens = x2.shape[0]
    blocks = tokens // TOK
    per_batch = seq // TOK
    x2_view = x2.rearrange("(n p) d -> n p d", p=P)
    out_view = out.rearrange("(n p) d -> n p d", p=P)
    F2_STEPS = JC + SUB - 1

    with ExitStack() as ctx:
        def sb(name, shape, dt=F32):
            return ctx.enter_context(nc.sbuf_tensor(name, shape, dt))

        def sem(name):
            return ctx.enter_context(nc.semaphore(name))

        w1_hi = sb("w1_hi", [P, KC, INTER], F32R)
        w1_lo = sb("w1_lo", [P, KC, INTER], F32R)
        w2_hi = sb("w2_hi", [P, JC, D], F32R)
        w2_lo = sb("w2_lo", [P, JC, D], F32R)
        modulation = sb("f_modulation", [P, batches, 2, KC])
        gate = sb("f_gate", [P, batches, D])
        bias = sb("f_bias", [P, D])

        w1_view = w1.rearrange("(k p) n -> p k n", p=P)
        w2_view = w2.rearrange("(j p) n -> p j n", p=P)
        weights = [(w1_view[:, :, q * D:(q + 1) * D], w1_hi[:, :, q * D:(q + 1) * D],
                    w1_lo[:, :, q * D:(q + 1) * D]) for q in range(INTER // D)]
        weights += [(w2_view[:, q:q + KC, :], w2_hi[:, q:q + KC, :], w2_lo[:, q:q + KC, :])
                    for q in range(0, JC, KC)]
        setup_block(nc, "sf", wmod, cT, b2, 3, 4, 5, batches, modulation[:, :, 0, :],
                    modulation[:, :, 1, :], gate[:],
                    bias[:], weights)

        ident = sb("f_ident", [P, P])
        b1 = sb("b1", [P, JC])
        current = sb("f_current", [P, 2, KC])
        half = sb("f_half", [P, SUB])
        xt = sb("x2t", [P, 2, SUB, D])
        stats = sb("f_stats", [P, SUB, 6])
        mean = sb("f_mean", [P, SUB])
        scratch = sb("f_scratch", [P, 2, SUB])
        var_eps = sb("f_var_eps", [P, SUB])
        rstd = sb("f_rstd", [P, SUB])
        xn = sb("xn", [P, SUB, D])
        hT = sb("h2T", [P, KC, TOK])
        h_hi = sb("h_hi", [P, KC, TOK], F32R)
        h_lo = sb("h_lo", [P, KC, TOK], F32R)
        hid = sb("hid", [P, 2, TOK])
        hid_hi = sb("hid_hi", [P, 2, TOK], F32R)
        hid_lo = sb("hid_lo", [P, 2, TOK], F32R)
        scaled = sb("f_scaled", [P, 2, D])
        ps = ctx.enter_context(nc.psum_tensor("f_ps", [P, 8, 512], F32))

        const_in = sem("f_const_in")
        half_set = sem("f_half_set")
        x2_in = sem("x2_in")
        stored = sem("stored")
        ln_stats = sem("f_ln_stats")
        ln_step = sem("f_ln_step")
        ln_rstd = sem("f_ln_rstd")
        xn_ready = sem("f_xn_ready")
        t_done = sem("f_t_done")
        h_ready = sem("f_h_ready")
        h_hi_set = sem("h_hi_set")
        h_lo_set = sem("h_lo_set")
        up_done = sem("up_done")
        relu_done = sem("relu_done")
        hid_hi_set = sem("hid_hi_set")
        hid_lo_set = sem("hid_lo_set")
        down_step = sem("down_step")
        sum_biased = sem("sum_biased")
        sum_scaled = sem("sum_scaled")
        out_ready = sem("out_ready")

        def chunk_used(i, j):
            if j < 0:
                j, i = j + JC, i - 1
            return F2_STEPS * i + (j + 1 if j < JC - 1 else F2_STEPS)

        def sum_done(i, s):
            return F2_STEPS * i + JC + s

        up_bank = [ps[:, 0], ps[:, 1]]
        t_bank = [ps[:, 2], ps[:, 3]]
        sums = [ps[:, 4 + s] for s in range(SUB)]

        block = ctx.enter_context(nc.Block())

        @block.sync
        def _(sp):
            sp.dma_start(ident[:], identity).then_inc(const_in, 16)
            sp.dma_start(b1[:], b1_in).then_inc(const_in, 16)

            def load(b):
                wait(sp, stored, 16 * (b - 1))
                wait(sp, xn_ready, SUB * b)
                sp.dma_start(xt[:, b % 2], x2_view[bass.ds(SUB * b, SUB)].rearrange("s p d -> p s d"))\
                  .then_inc(x2_in, 16)

            def store(b):
                sp.wait_ge(out_ready, SUB * (b + 1))
                sp.dma_start(out_view[bass.ds(SUB * b, SUB)].rearrange("s p d -> p s d"), xt[:, b % 2])\
                  .then_inc(stored, 16)

            load(0)
            load(1)
            store(0)
            with sp.Fori(1, blocks - 1) as i:
                load(i + 1)
                store(i)
            store(blocks - 1)
            sp.wait_ge(stored, 16 * blocks)

        @block.tensor
        def _(pe):
            def transpose_x(b, s):
                pe.wait_ge(xn_ready, SUB * b + s + 1)
                wait(pe, h_ready, SUB * b + s - 1)
                for c in range(KC):
                    last = pe.transpose(t_bank[s % 2][:, c * P:(c + 1) * P],
                                        xn[:, s, c * P:(c + 1) * P], ident[:])
                last.then_inc(t_done, 1)

            def up(i, j):
                wait(pe, relu_done, JC * i + j - 1)
                cols = slice(j * P, (j + 1) * P)
                for k in range(KC):
                    if j == 0:
                        pe.wait_ge(h_lo_set, KC * i + k + 1)
                    last = split_product(pe, up_bank[j % 2], w1_hi[:, k, cols], w1_lo[:, k, cols],
                                         h_hi[:, k, :], h_lo[:, k, :], k == 0, k == KC - 1)
                last.then_inc(up_done, 1)

            def down(i, j):
                pe.wait_ge(hid_lo_set, JC * i + j + 1)
                for s in range(SUB):
                    if j == 0:
                        wait(pe, sum_biased, SUB * (i - 1) + s + 1)
                    rows = slice(s * P, (s + 1) * P)
                    last = split_product(pe, sums[s], hid_hi[:, j % 2, rows],
                                         hid_lo[:, j % 2, rows], w2_hi[:, j, :], w2_lo[:, j, :],
                                         j == 0, j == JC - 1)
                    if j == JC - 1 or s == SUB - 1:
                        last.then_inc(down_step, 1)

            def body(i, after):
                for j in range(JC):
                    up(i, j)
                    if after and JC // 2 <= j < JC // 2 + SUB:
                        transpose_x(i + 1, j - JC // 2)
                    if j >= 2:
                        down(i, j - 2)
                down(i, JC - 2)
                down(i, JC - 1)

            pe.wait_ge(const_in, 32)
            for s in range(SUB):
                transpose_x(0, s)
            body(0, True)
            with pe.Fori(1, blocks - 1) as i:
                body(i, True)
            body(blocks - 1, False)

        @block.scalar
        def _(act):
            def modulated(b, s):
                act.wait_ge(t_done, SUB * b + s + 1)
                if s == 0:
                    wait(act, h_lo_set, KC * b)
                for c in range(KC):
                    last = act.activation(
                        hT[:, c, s * P:(s + 1) * P], t_bank[s % 2][:, c * P:(c + 1) * P],
                        ACT.Identity, bias=current[:, 0, c:c + 1],
                        scale=current[:, 1, c:c + 1])
                last.then_inc(h_ready, 1)

            def relu(i, j):
                wait(act, hid_lo_set, JC * i + j - 1)
                act.wait_ge(up_done, JC * i + j + 1)
                act.activation(hid[:, j % 2], up_bank[j % 2], ACT.Relu, bias=b1[:, j:j + 1])\
                   .then_inc(relu_done, 1)

            def body(i, after):
                for j in range(JC):
                    relu(i, j)
                    if after and JC // 2 <= j < JC // 2 + SUB:
                        modulated(i + 1, j - JC // 2)

            act.wait_ge(const_in, 32)
            for s in range(SUB):
                modulated(0, s)
            body(0, True)
            with act.Fori(1, blocks - 1) as i:
                body(i, True)
            body(blocks - 1, False)

        @block.vector
        def _(dve):
            def layer_norm_stats(b):
                dve.tensor_scalar(current[:], modulation[:, b // per_batch], 1.0, None, ALU.mult)
                dve.wait_ge(x2_in, 16 * (b + 1))
                for s in range(SUB):
                    dve.bn_stats(stats[:, s, :], xt[:, b % 2, s, :]).then_inc(ln_stats, 1)
                dve.wait_ge(ln_stats, SUB * (b + 1))
                moments_steps(dve, ln_step, MOMENT_STEPS * b, stats, mean[:], var_eps[:], scratch)

            def layer_norm(b):
                dve.wait_ge(ln_rstd, b + 1)
                wait(dve, t_done, SUB * b)
                for s in range(SUB):
                    dve.tensor_scalar(xn[:, s, :], xt[:, b % 2, s, :], mean[:, s:s + 1],
                                      rstd[:, s:s + 1], ALU.subtract, ALU.mult)\
                       .then_inc(xn_ready, 1)

            def split_h(b):
                dve.wait_ge(h_ready, SUB * (b + 1))
                wait(dve, up_done, JC * b)
                for c in range(KC):
                    dve.tensor_copy(h_hi[:, c, :], hT[:, c, :]).then_inc(h_hi_set, 1)
                    dve.wait_ge(h_hi_set, KC * b + c + 1)
                    dve.tensor_tensor(h_lo[:, c, :], hT[:, c, :], h_hi[:, c, :].bitcast(F32),
                                      ALU.subtract).then_inc(h_lo_set, 1)

            def hidden_hi(i, j):
                dve.wait_ge(relu_done, JC * i + j + 1)
                wait(dve, down_step, chunk_used(i, j - 2) if j >= 2 or not isinstance(i, int)
                     or i > 0 else 0)
                dve.tensor_copy(hid_hi[:, j % 2], hid[:, j % 2]).then_inc(hid_hi_set, 1)

            def sums_out(i):
                for s in range(SUB):
                    slot = scaled[:, s % 2]
                    dve.wait_ge(down_step, sum_done(i, s))
                    if s >= 2:
                        dve.wait_ge(out_ready, SUB * i + s - 1)
                    dve.tensor_tensor(slot, sums[s], bias[:], ALU.add).then_inc(sum_biased, 1)
                    dve.wait_ge(sum_biased, SUB * i + s + 1)
                    dve.tensor_tensor(slot, slot, gate[:, i // per_batch, :], ALU.mult)\
                       .then_inc(sum_scaled, 1)
                    dve.wait_ge(sum_scaled, SUB * i + s + 1)
                    part = xt[:, i % 2, s, :]
                    dve.tensor_tensor(part, part, slot, ALU.add).then_inc(out_ready, 1)

            def body(i, after):
                for j in range(JC):
                    hidden_hi(i, j)
                    if after and j == 3:
                        layer_norm_stats(i + 1)
                    if after and j == 4:
                        layer_norm(i + 1)
                if after:
                    split_h(i + 1)
                sums_out(i)

            layer_norm_stats(0)
            layer_norm(0)
            split_h(0)
            body(0, True)
            with dve.Fori(1, blocks - 1) as i:
                body(i, True)
            body(blocks - 1, False)

        @block.gpsimd
        def _(pool):
            def layer_norm_rstd(b):
                pool.wait_ge(ln_step, MOMENT_STEPS * (b + 1))
                pool.tensor_tensor(rstd[:], var_eps[:], half[:], ALU.pow).then_inc(ln_rstd, 1)

            def hidden_lo(i, j):
                pool.wait_ge(hid_hi_set, JC * i + j + 1)
                pool.tensor_tensor(hid_lo[:, j % 2], hid[:, j % 2], hid_hi[:, j % 2].bitcast(F32),
                                   ALU.subtract).then_inc(hid_lo_set, 1)

            def body(i, after):
                for j in range(JC):
                    hidden_lo(i, j)
                    if after and j == 3:
                        layer_norm_rstd(i + 1)

            pool.memset(half[:], -0.5).then_inc(half_set, 1)
            pool.wait_ge(half_set, 1)
            layer_norm_rstd(0)
            body(0, True)
            with pool.Fori(1, blocks - 1) as i:
                body(i, True)
            body(blocks - 1, False)


def build(nc, a):
    batches, seq, _ = a["x"].shape
    flat = "b t d -> (b t) d"
    x2 = nc.dram_tensor("x2", (batches * seq, D), F32).ap()
    attention(nc, a["x"].rearrange(flat), x2, a["mix"], [a[f"W_{m}"] for m in PROJ], a["W_out"],
              a["b_out"], a["gn"], a["cT"], a["wmod"], a["identity"], a["centering"],
              a["group_mean"], a["keep"], batches, seq)
    feed_forward(nc, x2, a["out"].rearrange(flat), a["W1"], a["W2"], a["b1"], a["b2"], a["cT"],
                 a["wmod"], a["identity"], batches, seq)


def kernel(**inputs):
    import numpy as np
    import concourse.bacc as bacc
    from concourse.bass_utils import run_bass_kernel_spmd

    def attn(name):
        return np.asarray(inputs[f"L0_attn_{name}"])

    def by_chunk(vector):
        return vector.reshape(-1, P).T

    x = attn("x")
    batches, seq, _ = x.shape
    arrays = {"x": x, "W1": inputs["L0_ffn_W1"], "W2": inputs["L0_ffn_W2"],
              "wmod": inputs["L0_wmod"], "W_out": attn("W_out").T}
    for m in PROJ:
        arrays[f"W_{m}"] = attn(f"W_{m}").T
    arrays["mix"] = np.concatenate([by_chunk(attn(f"x_{m}").reshape(D)) for m in PROJ], axis=1)
    arrays["gn"] = np.stack([by_chunk(attn("gn_w")), by_chunk(attn("gn_b"))], axis=1)
    arrays["cT"] = np.asarray(inputs["L0_c"]).T.reshape(KC, P, batches).transpose(1, 0, 2)
    arrays["b_out"] = attn("b_out").reshape(1, D)
    arrays["b1"] = by_chunk(np.asarray(inputs["L0_ffn_b1"]))
    arrays["b2"] = np.asarray(inputs["L0_ffn_b2"]).reshape(1, D)
    same = np.kron(np.eye(GPC), np.full((GROUP, GROUP), 1.0 / GROUP))
    keep = np.ones((P, batches * seq // TOK + 1))
    keep[:, ::seq // TOK] = 0.0
    arrays["identity"] = np.eye(P)
    arrays["centering"] = np.eye(P) - same
    arrays["group_mean"] = same[:, ::GROUP]
    arrays["keep"] = keep
    arrays = {n: np.ascontiguousarray(v, np.float32) for n, v in arrays.items()}

    nc = bacc.Bacc("TRN2", target_bir_lowering=False, num_devices=1)
    aps = {n: nc.dram_tensor(f"in_{n}", v.shape, F32, kind="ExternalInput").ap()
           for n, v in arrays.items()}
    aps["out"] = nc.dram_tensor("out", x.shape, F32, kind="ExternalOutput").ap()
    build(nc, aps)
    result = run_bass_kernel_spmd(nc, [{f"in_{n}": v for n, v in arrays.items()}], core_ids=[0])
    return result.results[0]["out"]
```

```python
from contextlib import ExitStack

import concourse.bass as bass
from concourse import mybir
from concourse.alu_op_type import AluOpType as ALU

F32 = mybir.dt.float32
F32R = mybir.dt.float32r
I32 = mybir.dt.int32
ACT = mybir.ActivationFunctionType

P = 128
D = 512
KC = D // P
TOK = 512
SUB = TOK // P
HEADS = 16
GROUP = D // HEADS
GPC = P // GROUP
INTER = 2048
JC = INTER // P
LN_EPS = 1e-5
GN_EPS = 0.00064
GATE_MIN = 0.25

PROJ = ["k", "a", "v", "w", "r", "g"]
NP = len(PROJ)
PIECES = NP * KC
HI_RING = 4
F32_RING = 3
GATE_RING = 3
PROJ_BANKS = 6
AUX = [6, 7]
STEPS = 2 * KC - 1


def wait(engine, semaphore, value):
    if not isinstance(value, int) or value > 0:
        engine.wait_ge(semaphore, value)


def split_product(pe, acc, a_hi, a_lo, b_hi, b_lo, first, last):
    pe.matmul(acc, a_hi, b_hi, start=first, stop=False)
    pe.matmul(acc, a_hi, b_lo, start=False, stop=False)
    return pe.matmul(acc, a_lo, b_hi, start=False, stop=last)


def moments_steps(dve, step, steps_before, stats, mean, var_eps, scratch):
    mean_e, mean_o, m2_e, m2_o = (stats[:, :, q] for q in (1, 4, 2, 5))
    diff, m2 = scratch[:, 0, :], scratch[:, 1, :]
    dve.tensor_tensor(diff, mean_e, mean_o, ALU.subtract).then_inc(step, 1)
    dve.scalar_tensor_tensor(m2, m2_e, D * LN_EPS, m2_o, ALU.add, ALU.add).then_inc(step, 1)
    dve.tensor_tensor(mean, mean_e, mean_o, ALU.add).then_inc(step, 1)
    dve.wait_ge(step, steps_before + 3)
    dve.scalar_tensor_tensor(diff, diff, 0.25, diff, ALU.mult, ALU.mult).then_inc(step, 1)
    dve.tensor_scalar(mean, mean, 0.5, None, ALU.mult).then_inc(step, 1)
    dve.wait_ge(step, steps_before + 5)
    dve.scalar_tensor_tensor(var_eps, m2, 1.0 / D, diff, ALU.mult, ALU.add).then_inc(step, 1)


MOMENT_STEPS = 6


def inverse_root(dve, step, steps_before, value, root, bits, scratch):
    count = [steps_before]

    def then(instruction):
        instruction.then_inc(step, 1)
        count[0] += 1
        dve.wait_ge(step, count[0])

    then(dve.tensor_scalar(bits, value.bitcast(I32), 1, None, ALU.logical_shift_right))
    then(dve.tensor_scalar(bits, bits, -1.0, float(0x5F3759DF), ALU.mult, ALU.add))
    for _ in range(NEWTON):
        then(dve.tensor_tensor(scratch, root, root, ALU.mult))
        then(dve.scalar_tensor_tensor(scratch, scratch, -0.5, value, ALU.mult, ALU.mult))
        then(dve.scalar_tensor_tensor(root, scratch, 1.5, root, ALU.add, ALU.mult))


NEWTON = 3
ROOT_STEPS = 2 + 3 * NEWTON


def under(nc, name, shape):
    with nc.sbuf_tensor(name, shape, F32) as tile:
        return tile


def weight_hi(act, arrived, raw, tile_hi, hi_set):
    act.wait_ge(arrived, 16)
    act.activation(tile_hi, raw, ACT.Copy).then_inc(hi_set, 1)


def first_weight_hi(dve, arrived, raw, tile_hi, hi_set):
    dve.wait_ge(arrived, 16)
    dve.tensor_copy(tile_hi, raw).then_inc(hi_set, 1)


def weight_lo(engine, hi_set, count, raw, tile_hi, tile_lo, ready):
    engine.wait_ge(hi_set, count)
    engine.tensor_tensor(tile_lo, raw, tile_hi.bitcast(F32), ALU.subtract)\
          .then_inc(ready, 1)


def modulation_product(pe, columns, wmod_group, silu, batches, done):
    for c in range(KC):
        for k in range(KC):
            last = pe.matmul(columns[:, c * batches:(c + 1) * batches],
                             wmod_group[:, k, c * P:(c + 1) * P], silu[:, k, :],
                             start=k == 0, stop=k == KC - 1)
    last.then_inc(done, 1)


def modulation_out(dve, target, columns, batches, done):
    for q in range(2):
        got = columns[:, q * KC * batches:(q + 1) * KC * batches]\
            .rearrange("p (c b) -> p c b", b=batches)
        for b in range(batches):
            last = dve.tensor_scalar(target[:, b, q, :], got[:, :, b], float(q), None, ALU.add)
    last.then_inc(done, 1)


def gate_product(pe, rows, wmod_group, silu, batches, done):
    for b in range(batches):
        for k in range(KC):
            last = pe.matmul(rows[b], silu[:, k, b:b + 1].broadcast_to([P, P]),
                             wmod_group[:, k, :], start=k == 0, stop=k == KC - 1)
    last.then_inc(done, 1)


def gate_out(dve, gate, raw, rows, batches, step):
    for b in range(batches):
        dve.tensor_copy(raw[:, b, :], rows[b]).then_inc(step, 1)
    dve.wait_ge(step, batches)
    dve.scalar_tensor_tensor(gate, raw, -1.0, raw, ALU.mult, ALU.max).then_inc(step, 1)
    dve.wait_ge(step, batches + 1)
    dve.tensor_scalar(gate, gate, GATE_MIN, None, ALU.max).then_inc(step, 1)
    dve.wait_ge(step, batches + 2)
    dve.scalar_tensor_tensor(raw, raw, 0.0, gate, ALU.is_ge, ALU.mult).then_inc(step, 1)
    dve.wait_ge(step, batches + 3)
    dve.scalar_tensor_tensor(gate, raw, 2.0, gate, ALU.mult, ALU.subtract).then_inc(step, 1)
    dve.wait_ge(step, batches + 4)


def attention(nc, x, x2, mixes, w_proj, w_out, b_out, gn, cT_in, wmod, silu, modulation,
              identity, centering, group_mean, keep_in, batches, seq):
    tokens = x.shape[0]
    blocks = tokens // TOK
    per_batch = seq // TOK
    x_view = x.rearrange("(n p) d -> n p d", p=P)
    x2_view = x2.rearrange("(n p) d -> n p d", p=P)

    with ExitStack() as ctx:
        def sb(name, shape, dt=F32):
            return ctx.enter_context(nc.sbuf_tensor(name, shape, dt))

        def sem(name):
            return ctx.enter_context(nc.semaphore(name))

        w_hi = sb("w_hi", [P, NP + 1, KC, D], F32R)
        w_raw = under(nc, "w_raw", [P, NP + 1, KC, D])
        w_lo = sb("w_lo", [P, NP + 1, KC, D], F32R)
        gate = sb("gate", [P, batches, D])
        bias = sb("bias", [P, D])
        cT = sb("cT", [P, KC, batches])
        sig = sb("sig", [P, KC, batches])

        ident = sb("ident", [P, P])
        center = sb("center", [P, P])
        g_mean = sb("g_mean", [P, GPC])
        mix = sb("mix", [P, PIECES])
        unmix = sb("unmix", [P, PIECES])
        gn_wb = sb("gn_wb", [P, 2, KC])
        keep = sb("keep", [P, blocks + 1])
        current = sb("current", [P, 2, KC])
        keep_now = sb("keep_now", [P, 1])
        half = sb("half", [P, SUB])
        state = sb("state", [P, KC])

        xt = sb("xt", [P, SUB, D])
        stats = sb("stats", [P, SUB, 6])
        mean = sb("mean", [P, SUB])
        scratch = sb("scratch", [P, 2, SUB])
        var_eps = sb("var_eps", [P, SUB])
        rstd = sb("rstd", [P, SUB])
        hT = sb("hT", [P, KC, 1 + TOK])
        mixed_in = sb("mixed_in", [P, F32_RING, TOK])
        in_hi = sb("in_hi", [P, HI_RING, TOK], F32R)
        in_lo = sb("in_lo", [P, HI_RING, TOK], F32R)
        u = sb("u", [P, KC, TOK])
        gates = sb("gates", [P, GATE_RING, TOK])
        g_sig = sb("g_sig", [P, KC, TOK])
        square = rstd_wide = scaled = sb("square_wide_scaled", [P, 2, TOK])
        g_var = sb("g_var", [P, SUB * HEADS])
        g_rstd = sb("g_rstd", [P, SUB * HEADS])
        g_scratch = sb("g_scratch", [P, SUB * HEADS])
        wmod_y = under(nc, "wmod_y", [P, 2, KC, D])
        y_hi = sb("y_hi", [P, KC, TOK], F32R)
        y_lo = sb("y_lo", [P, KC, TOK], F32R)
        wmod_tile = {"scale": wmod_y[:, 0], "shift": wmod_y[:, 1], "gate": g_sig[:]}
        res = sb("res", [P, 2, D])
        ps = ctx.enter_context(nc.psum_tensor("ps", [P, 8, 512], F32))

        c_in = sem("c_in")
        sig_ready = sem("sig_ready")
        silu_ready = sem("silu_ready")
        wmod_in = {q: sem(f"wmod_in_{q}") for q in wmod_tile}
        mod_done = sem("mod_done")
        mod_set = sem("mod_set")
        gate_step = sem("gate_step")
        bias_in = sem("bias_in")
        w_in = [sem(f"w_in{m}") for m in range(NP + 1)]
        w0_hi_set = sem("w0_hi_set")
        w_hi_set = sem("w_hi_set")
        w_ready = [sem(f"w_ready{m}") for m in range(NP + 1)]
        current_set = sem("current_set")
        const_in = sem("const_in")
        const_set = sem("const_set")
        unmix_set = sem("unmix_set")
        x_in = sem("x_in")
        ln_stats = sem("ln_stats")
        ln_step = sem("ln_step")
        ln_rstd = sem("ln_rstd")
        xn_ready = sem("xn_ready")
        t_done = sem("t_done")
        h_ready = sem("h_ready")
        carried = sem("carried")
        prev_scaled = sem("prev_scaled")
        mix_ready = sem("mix_ready")
        hi_ready = sem("hi_ready")
        lo_ready = sem("lo_ready")
        proj_step = sem("proj_step")
        act_out = sem("act_out")
        v_out = sem("v_out")
        gate_used = sem("gate_used")
        state_kept = sem("state_kept")
        center_done = sem("center_done")
        centered = sem("centered")
        squared = sem("squared")
        var_done = sem("var_done")
        g_var_set = sem("g_var_set")
        root_step = sem("root_step")
        wide_set = sem("wide_set")
        wide_done = sem("wide_done")
        normed = sem("normed")
        gated = sem("gated")
        y_hi_set = sem("y_hi_set")
        y_lo_set = sem("y_lo_set")
        out_done = sem("out_done")
        out_biased = sem("out_biased")
        out_scaled = sem("out_scaled")
        res_in = [sem(f"res_in{s}") for s in range(2)]
        x2_ready = sem("x2_ready")
        x2_out = [sem(f"x2_out{s}") for s in range(2)]

        def aux(n):
            return ps[:, AUX[n % 2]]

        def proj_bank(n):
            return ps[:, n % PROJ_BANKS]

        def input_used(i, n):
            if n < 0:
                n, i = n + PIECES, i - 1
            m, k = divmod(n, KC)
            return STEPS * NP * i + STEPS * m + (k + 1 if k < KC - 1 else STEPS)

        def output_done(i, m, o):
            return STEPS * NP * i + STEPS * m + KC + o

        columns = {0: ps[:, PROJ_BANKS - 1], 1: aux(0)}

        def modulation_of(phase):
            return columns[phase][:, :KC * batches], columns[phase][:, KC * batches:]

        w_view = [w.rearrange("(k p) n -> p k n", p=P) for w in (*w_proj, w_out)]
        wmod_view = wmod.rearrange("(k p) n -> p k n", p=P)
        gate_rows = [aux(b) for b in range(batches)]
        block = ctx.enter_context(nc.Block())

        @block.sync
        def _(sp):
            def load_wmod(name, q):
                sp.dma_start(wmod_tile[name], wmod_view[:, :, q * D:(q + 1) * D])\
                  .then_inc(wmod_in[name], 16)

            def load_weight(m):
                sp.dma_start(w_raw[:, m], w_view[m]).then_inc(w_in[m], 16)

            sp.dma_start(cT[:], cT_in).then_inc(c_in, 16)
            load_wmod("scale", 1)
            load_wmod("shift", 0)
            loads = [(ident, identity), (center, centering), (g_mean, group_mean),
                     (mix, mixes), (gn_wb, gn), (keep, keep_in)]
            for tile, source in loads:
                sp.dma_start(tile[:], source).then_inc(const_in, 16)

            def load_x(b):
                wait(sp, t_done, SUB * b)
                sp.dma_start(xt[:], x_view[bass.ds(SUB * b, SUB)].rearrange("s p d -> p s d"))\
                  .then_inc(x_in, 16)

            def residual(j):
                def load(s):
                    wait(sp, x2_out[s % 2], 16 * (2 * j + s // 2))
                    sp.dma_start(res[:, s % 2], x_view[SUB * j + s]).then_inc(res_in[s % 2], 16)

                def store(s):
                    sp.wait_ge(x2_ready, SUB * j + s + 1)
                    sp.dma_start(x2_view[SUB * j + s], res[:, s % 2]).then_inc(x2_out[s % 2], 16)

                load(0)
                load(1)
                for s in range(2, SUB):
                    store(s - 2)
                    load(s)
                store(SUB - 2)
                store(SUB - 1)

            def body(i, before, after):
                if after:
                    load_x(i + 1)
                if before:
                    residual(i - 1)

            load_x(0)
            sp.dma_start(bias[:], b_out.partition_broadcast(P)).then_inc(bias_in, 16)
            load_weight(0)
            load_weight(1)
            load_wmod("gate", 2)
            load_weight(2)
            load_weight(3)
            load_x(1)
            load_weight(4)
            load_weight(5)
            sp.wait_ge(mod_done, 2)
            load_wmod("scale", 4)
            load_wmod("shift", 3)
            load_weight(NP)
            body(1, True, True)
            with sp.Fori(2, blocks - 1) as i:
                body(i, True, True)
            body(blocks - 1, True, False)
            residual(blocks - 1)
            for s in range(2):
                sp.wait_ge(x2_out[s], 16 * 2 * blocks)

        @block.tensor
        def _(pe):
            def bank_free(i, n):
                n -= PROJ_BANKS
                if n < 0:
                    n, i = n + PIECES, i - 1
                m, o = divmod(n, KC)
                if PROJ[m] == "v":
                    wait(pe, v_out, KC * i + o + 1)
                else:
                    wait(pe, act_out, (PIECES - KC) * i + n + 1 - (KC if m > 2 else 0))

            def modulate(phase):
                shift, scale = modulation_of(phase)
                for name, target in (("scale", scale), ("shift", shift)):
                    pe.wait_ge(wmod_in[name], 16 * (phase + 1))
                    modulation_product(pe, target, wmod_tile[name], silu, batches, mod_done)

            def project(i, m, k, between=()):
                n = m * KC + k
                slot = n % HI_RING
                if k == 0 and isinstance(i, int) and i == 0:
                    pe.wait_ge(w_ready[m], 1)
                pe.wait_ge(lo_ready, PIECES * i + n + 1)
                for o in range(KC):
                    if k == 0:
                        bank_free(i, m * KC + o)
                    cols = slice(o * P, (o + 1) * P)
                    last = split_product(pe, proj_bank(m * KC + o), w_hi[:, m, k, cols],
                                         w_lo[:, m, k, cols], in_hi[:, slot], in_lo[:, slot],
                                         k == 0, k == KC - 1)
                    if k == KC - 1 or o == KC - 1:
                        last.then_inc(proj_step, 1)
                    if o < len(between):
                        between[o]()

            def transpose_x(b, subs):
                for s in subs:
                    pe.wait_ge(xn_ready, SUB * b + s + 1)
                    if s < 2 and isinstance(b, int) and b < 2:
                        wait(pe, h_ready, SUB * (b - 1) + s + 3)
                    elif s < 2:
                        pe.wait_ge(out_biased, SUB * (b - 2) + s + 3)
                    else:
                        pe.wait_ge(h_ready, SUB * b + s - 1)
                    for c in range(KC):
                        last = pe.transpose(aux(s + 1)[:, c * P:(c + 1) * P],
                                            xt[:, s, c * P:(c + 1) * P], ident[:])
                    last.then_inc(t_done, 1)

            def center_chunk(i, c, after):
                pe.wait_ge(gate_used, 3 * KC * i + 2 * KC + c + 1)
                if c >= 2:
                    pe.wait_ge(centered, KC * i + c - 1)
                elif after:
                    pe.wait_ge(h_ready, SUB * (i + 1) + c + 3)
                else:
                    pe.wait_ge(out_biased, SUB * (i - 1) + c + 3)
                pe.matmul(aux(c + 1), center[:], u[:, c, :], start=True, stop=True)\
                  .then_inc(center_done, 1)

            def variance(i, c):
                pe.wait_ge(squared, KC * i + c + 1)
                if c == 0:
                    pe.wait_ge(centered, KC * i + KC)
                for s in range(SUB):
                    at = s * HEADS + c * GPC
                    last = pe.matmul(aux(0)[:, at:at + GPC], square[:, c % 2, s * P:(s + 1) * P],
                                     g_mean[:], start=True, stop=True)
                last.then_inc(var_done, 1)

            def widen(j, s):
                pe.wait_ge(wide_set, SUB * j + s + 1)
                if s == 1:
                    pe.wait_ge(g_var_set, j + 1)
                if s >= 2:
                    pe.wait_ge(normed, SUB * j + s - 1)
                for c in range(KC):
                    last = pe.transpose(aux(s + 1)[:, c * P:(c + 1) * P],
                                        rstd_wide[:, s % 2, c * P:(c + 1) * P], ident[:])
                last.then_inc(wide_done, 1)

            def output(j):
                if isinstance(j, int) and j == 0 or blocks == 1:
                    pe.wait_ge(w_ready[NP], 1)
                pe.wait_ge(y_lo_set, KC * (j + 1))
                for s in range(SUB):
                    if s < 2:
                        pe.wait_ge(normed, SUB * j + s + 3)
                    else:
                        pe.wait_ge(out_biased, SUB * j + s - 1)
                    for k in range(KC):
                        rows = slice(s * P, (s + 1) * P)
                        last = split_product(pe, aux(s + 1), y_hi[:, k, rows], y_lo[:, k, rows],
                                             w_hi[:, NP, k, :], w_lo[:, NP, k, :],
                                             k == 0, k == KC - 1)
                    last.then_inc(out_done, 1)

            def body(i, before, after):
                project(i, 0, 0)
                project(i, 0, 1)
                if before:
                    widen(i - 1, 0)
                    widen(i - 1, 1)
                    project(i, 0, 2, between=(lambda: widen(i - 1, 2), lambda: widen(i - 1, 3)))
                else:
                    project(i, 0, 2)
                project(i, 0, 3)
                first = not before
                if first:
                    pe.wait_ge(mod_set, 1)
                for k in range(KC):
                    project(i, 1, k)
                if before:
                    output(i - 1)
                if first:
                    pe.wait_ge(wmod_in["gate"], 16)
                    pe.wait_ge(h_ready, SUB)
                    gate_product(pe, gate_rows, wmod_tile["gate"], silu, batches, mod_done)
                for m in (2, 3, 4):
                    for k in range(KC):
                        project(i, m, k)
                        if after and (m, k) == (4, KC - 2):
                            transpose_x(i + 1, (0, 1))
                    if first and m == 3:
                        pe.wait_ge(gate_step, batches)
                        modulate(1)
                        pe.wait_ge(mod_set, 2)
                if after:
                    transpose_x(i + 1, (2, 3))
                for k in range(KC):
                    project(i, 5, k)
                    if k < 2:
                        center_chunk(i, 2 * k, after)
                        center_chunk(i, 2 * k + 1, after)
                    else:
                        variance(i, 2 * k - 4)
                        variance(i, 2 * k - 3)

            pe.wait_ge(silu_ready, 1)
            modulate(0)
            pe.wait_ge(const_in, 6 * 16)
            transpose_x(0, range(SUB))
            body(0, False, True)
            with pe.Fori(1, blocks - 1) as i:
                body(i, True, True)
            body(blocks - 1, True, False)
            for s in range(SUB):
                widen(blocks - 1, s)
            output(blocks - 1)

        @block.scalar
        def _(act):
            def scale_prev(b, m, c):
                n = m * KC + c
                if n == 0:
                    act.wait_ge(h_ready, SUB * (b + 1))
                    wait(act, carried, b)
                wait(act, lo_ready, PIECES * b + n + 1 - F32_RING)
                act.activation(mixed_in[:, n % F32_RING], hT[:, c, 0:TOK], ACT.Copy,
                               scale=mix[:, n:n + 1]).then_inc(prev_scaled, 1)

            def out_of_psum(i, m):
                name = PROJ[m]
                func = ACT.Tanh if name == "k" else ACT.Sigmoid
                for o in range(KC):
                    if name == "k":
                        wait(act, y_lo_set, KC * (i - 1) + o + 1)
                        target = u[:, o, :]
                    elif name == "g":
                        wait(act, gated, KC * (i - 1) + o + 1)
                        target = g_sig[:, o, :]
                    else:
                        n = {"a": 0, "w": 1, "r": 2}[name] * KC + o
                        wait(act, gate_used, 3 * KC * i + n + 1 - GATE_RING)
                        target = gates[:, n % GATE_RING]
                    act.wait_ge(proj_step, output_done(i, m, o))
                    act.activation(target, proj_bank(m * KC + o), func,
                                   scale=-1.0 if name == "w" else 1.0).then_inc(act_out, 1)

            def split_hi(m):
                weight_hi(act, w_in[m], w_raw[:, m], w_hi[:, m], w_hi_set)

            def modulated(b, subs):
                act.wait_ge(current_set, b + 1)
                wait(act, mix_ready, PIECES * b)
                if 0 in subs and not (isinstance(b, int) and b == 0):
                    act.activation(hT[:, :, 0:1], hT[:, :, TOK:TOK + 1], ACT.Copy,
                                   scale=keep_now[:]).then_inc(carried, 1)
                for s in subs:
                    act.wait_ge(t_done, SUB * b + s + 1)
                    if s == SUB - 1:
                        wait(act, carried, b)
                    for c in range(KC):
                        last = act.activation(
                            hT[:, c, 1 + s * P:1 + (s + 1) * P], aux(s + 1)[:, c * P:(c + 1) * P],
                            ACT.Identity, bias=current[:, 0, c:c + 1],
                            scale=current[:, 1, c:c + 1])
                    last.then_inc(h_ready, 1)

            def center_out(i, c):
                act.wait_ge(center_done, KC * i + c + 1)
                act.activation(u[:, c, :], aux(c + 1), ACT.Copy).then_inc(centered, 1)

            def square_chunk(i, c):
                act.wait_ge(centered, KC * i + c + 1)
                if c >= 2:
                    act.wait_ge(var_done, KC * i + c - 1)
                act.activation(square[:, c % 2], u[:, c, :], ACT.Square).then_inc(squared, 1)

            def body(i, before, after):
                for c in range(KC):
                    scale_prev(i, 1, c)
                out_of_psum(i, 0)
                for m in range(1, NP - 1):
                    if not before:
                        split_hi(m + 1)
                    for c in range(KC):
                        scale_prev(i, m + 1, c)
                    if PROJ[m] == "r" and after:
                        modulated(i + 1, (0, 1))
                    if PROJ[m] != "v":
                        out_of_psum(i, m)
                if after:
                    modulated(i + 1, (2, 3))
                for c in range(KC):
                    if after:
                        scale_prev(i + 1, 0, c)
                    center_out(i, c)
                    if c == 1:
                        square_chunk(i, 0)
                        square_chunk(i, 1)
                square_chunk(i, 2)
                square_chunk(i, 3)
                out_of_psum(i, NP - 1)
                if not before:
                    split_hi(NP)

            act.wait_ge(c_in, 16)
            act.activation(sig[:], cT[:], ACT.Sigmoid).then_inc(sig_ready, 1)
            act.wait_ge(const_in, 6 * 16)
            act.wait_ge(const_set, 3)
            modulated(0, range(SUB))
            for c in range(F32_RING):
                scale_prev(0, 0, c)
            split_hi(1)
            scale_prev(0, 0, KC - 1)
            body(0, False, True)
            with act.Fori(1, blocks - 1) as i:
                body(i, True, True)
            body(blocks - 1, True, False)

        @block.vector
        def _(dve):
            def split_lo(m):
                weight_lo(dve, w_hi_set, m, w_raw[:, m], w_hi[:, m], w_lo[:, m], w_ready[m])

            def take_modulation(phase):
                dve.wait_ge(mod_done, (2, 5)[phase])
                modulation_out(dve, modulation[:, phase], columns[phase], batches, mod_set)
                dve.wait_ge(mod_set, phase + 1)

            def set_current(b):
                dve.tensor_scalar(keep_now[:], keep[:, bass.ds(b, 1)], 1.0, None, ALU.mult)
                dve.tensor_scalar(current[:], modulation[:, 0, b // per_batch], 1.0, None, ALU.mult)\
                   .then_inc(current_set, 1)

            def layer_norm_stats(b, s):
                dve.wait_ge(x_in, 16 * (b + 1))
                dve.bn_stats(stats[:, s, :], xt[:, s, :]).then_inc(ln_stats, 1)

            def layer_norm_moments(b):
                dve.wait_ge(ln_stats, SUB * (b + 1))
                moments_steps(dve, ln_step, MOMENT_STEPS * b, stats, mean[:], var_eps[:], scratch)

            def layer_norm(b):
                dve.wait_ge(ln_rstd, b + 1)
                for s in range(SUB):
                    dve.tensor_scalar(xt[:, s, :], xt[:, s, :], mean[:, s:s + 1],
                                      rstd[:, s:s + 1], ALU.subtract, ALU.mult)\
                       .then_inc(xn_ready, 1)

            def mix_piece(b, m, c):
                n = m * KC + c
                made = mixed_in[:, n % F32_RING]
                dve.wait_ge(prev_scaled, PIECES * b + n + 1)
                dve.scalar_tensor_tensor(made, hT[:, c, 1:1 + TOK], unmix[:, n:n + 1], made,
                                         ALU.mult, ALU.add).then_inc(mix_ready, 1)

            def hi_piece(b, m, c):
                n = m * KC + c
                dve.wait_ge(mix_ready, PIECES * b + n + 1)
                wait(dve, proj_step, input_used(b, n - HI_RING) if n >= HI_RING or
                     not isinstance(b, int) or b > 0 else 0)
                dve.tensor_copy(in_hi[:, n % HI_RING], mixed_in[:, n % F32_RING])\
                   .then_inc(hi_ready, 1)

            def input_and_use(i, m, use):
                mix_piece(i, m, 0)
                hi_piece(i, m, 0)
                mix_piece(i, m, 1)
                hi_piece(i, m, 1)
                mix_piece(i, m, 2)
                mix_piece(i, m, 3)
                hi_piece(i, m, 2)
                use(i, 0)
                use(i, 1)
                hi_piece(i, m, 3)
                use(i, 2)
                use(i, 3)

            def use_a(i, c):
                dve.wait_ge(act_out, 5 * KC * i + KC + c + 1)
                dve.tensor_tensor(u[:, c, :], u[:, c, :], gates[:, c % GATE_RING], ALU.mult)\
                   .then_inc(gate_used, 1)

            def use_v(i, c):
                dve.wait_ge(proj_step, output_done(i, 2, c))
                dve.wait_ge(gate_used, 3 * KC * i + c + 1)
                dve.tensor_tensor(u[:, c, :], u[:, c, :], proj_bank(2 * KC + c), ALU.mult)\
                   .then_inc(v_out, 1)

            def scan(i, c):
                dve.wait_ge(act_out, 5 * KC * i + 2 * KC + c + 1)
                dve.wait_ge(v_out, KC * i + c + 1)
                wait(dve, state_kept, KC * (i - 1) + c + 1)
                dve.tensor_tensor_scan(u[:, c, :], gates[:, (KC + c) % GATE_RING], u[:, c, :],
                                       state[:, c:c + 1], ALU.mult, ALU.add)\
                   .then_inc(gate_used, 1)
                dve.wait_ge(gate_used, 3 * KC * i + KC + c + 1)
                dve.tensor_scalar(state[:, c:c + 1], u[:, c, TOK - 1:TOK],
                                  keep[:, bass.ds(i + 1, 1)], None, ALU.mult)\
                   .then_inc(state_kept, 1)

            def use_r(i, c):
                dve.wait_ge(act_out, 5 * KC * i + 3 * KC + c + 1)
                dve.wait_ge(state_kept, KC * i + c + 1)
                dve.tensor_tensor(u[:, c, :], u[:, c, :], gates[:, (2 * KC + c) % GATE_RING],
                                  ALU.mult).then_inc(gate_used, 1)

            def group_variance(j):
                dve.wait_ge(var_done, KC * (j + 1))
                dve.tensor_scalar(g_var[:], aux(0)[:, 0:SUB * HEADS], GN_EPS, None, ALU.add)\
                   .then_inc(g_var_set, 1)
                dve.wait_ge(g_var_set, j + 1)
                inverse_root(dve, root_step, ROOT_STEPS * j, g_var[:], g_rstd[:],
                             g_rstd[:].bitcast(I32), g_scratch[:])

            def wide(j, s):
                if s >= 2:
                    dve.wait_ge(wide_done, SUB * j + s - 1)
                dve.tensor_copy(
                    rstd_wide[:, s % 2].rearrange("p (g c) -> p g c", c=GROUP),
                    g_rstd[:, s * HEADS:(s + 1) * HEADS].unsqueeze(2)
                    .broadcast_to([P, HEADS, GROUP])).then_inc(wide_set, 1)

            def normalise(j, s):
                dve.wait_ge(wide_done, SUB * j + s + 1)
                for c in range(KC):
                    part = u[:, c, s * P:(s + 1) * P]
                    last = dve.scalar_tensor_tensor(part, aux(s + 1)[:, c * P:(c + 1) * P],
                                                    gn_wb[:, 0, c:c + 1], part, ALU.mult, ALU.mult)
                last.then_inc(normed, 1)

            def gate_y(j, c):
                dve.wait_ge(normed, SUB * (j + 1))
                dve.wait_ge(act_out, 5 * KC * j + 4 * KC + c + 1)
                dve.scalar_tensor_tensor(u[:, c, :], u[:, c, :], gn_wb[:, 1, c:c + 1],
                                         g_sig[:, c, :], ALU.add, ALU.mult).then_inc(gated, 1)
                dve.wait_ge(gated, KC * j + c + 1)
                dve.tensor_copy(y_hi[:, c, :], u[:, c, :]).then_inc(y_hi_set, 1)

            def scale_output(j, s):
                slot = scaled[:, s % 2]
                dve.wait_ge(out_done, SUB * j + s + 1)
                if s >= 2:
                    dve.wait_ge(x2_ready, SUB * j + s - 1)
                dve.tensor_tensor(slot, aux(s + 1), bias[:], ALU.add).then_inc(out_biased, 1)
                dve.wait_ge(out_biased, SUB * j + s + 1)
                dve.tensor_tensor(slot, slot, gate[:, j // per_batch, :], ALU.mult)\
                   .then_inc(out_scaled, 1)

            def body(i, before, after):
                j = i - 1
                if before:
                    group_variance(j)
                    wide(j, 0)
                    wide(j, 1)
                mix_piece(i, 1, 0)
                hi_piece(i, 1, 0)
                mix_piece(i, 1, 1)
                if before:
                    wide(j, 2)
                    normalise(j, 0)
                    wide(j, 3)
                    normalise(j, 1)
                hi_piece(i, 1, 1)
                if before:
                    normalise(j, 2)
                    normalise(j, 3)
                    gate_y(j, 0)
                    gate_y(j, 1)
                mix_piece(i, 1, 2)
                mix_piece(i, 1, 3)
                hi_piece(i, 1, 2)
                if before:
                    gate_y(j, 2)
                    gate_y(j, 3)
                hi_piece(i, 1, 3)
                if not before:
                    split_lo(2)
                input_and_use(i, 2, use_a)
                if not before:
                    dve.wait_ge(mod_done, 3)
                    gate_out(dve, gate[:], wmod_tile["gate"][:, 0:batches, :], gate_rows, batches,
                             gate_step)
                    dve.wait_ge(bias_in, 16)
                for s in range(SUB):
                    if before:
                        scale_output(j, s)
                    if after:
                        layer_norm_stats(i + 1, s)
                if after:
                    layer_norm_moments(i + 1)
                    set_current(i + 1)
                input_and_use(i, 3, use_v)
                if after:
                    layer_norm(i + 1)
                if not before:
                    split_lo(4)
                input_and_use(i, 4, scan)
                if not before:
                    take_modulation(1)
                input_and_use(i, 5, use_r)
                if after:
                    for c in range(KC):
                        mix_piece(i + 1, 0, c)
                        hi_piece(i + 1, 0, c)
                if not before:
                    split_lo(NP)

            dve.wait_ge(sig_ready, 1)
            dve.tensor_tensor(silu[:], cT[:], sig[:], ALU.mult).then_inc(silu_ready, 1)
            dve.wait_ge(const_in, 6 * 16)
            dve.wait_ge(const_set, 3)
            dve.tensor_scalar(unmix[:], mix[:], -1.0, 1.0, ALU.mult, ALU.add).then_inc(unmix_set, 1)
            dve.wait_ge(unmix_set, 1)
            for s in range(SUB):
                layer_norm_stats(0, s)
            layer_norm_moments(0)
            layer_norm(0)
            take_modulation(0)
            set_current(0)
            first_weight_hi(dve, w_in[0], w_raw[:, 0], w_hi[:, 0], w0_hi_set)
            for c in range(KC):
                mix_piece(0, 0, c)
                hi_piece(0, 0, c)
            body(0, False, True)
            with dve.Fori(1, blocks - 1) as i:
                body(i, True, True)
            body(blocks - 1, True, False)
            group_variance(blocks - 1)
            for s in range(SUB):
                wide(blocks - 1, s)
                normalise(blocks - 1, s)
            for c in range(KC):
                gate_y(blocks - 1, c)
            for s in range(SUB):
                scale_output(blocks - 1, s)

        @block.gpsimd
        def _(pool):
            def lo_piece(b, m, c):
                n = m * KC + c
                pool.wait_ge(hi_ready, PIECES * b + n + 1)
                pool.tensor_tensor(in_lo[:, n % HI_RING], mixed_in[:, n % F32_RING],
                                   in_hi[:, n % HI_RING].bitcast(F32), ALU.subtract)\
                    .then_inc(lo_ready, 1)

            def layer_norm_rstd(b):
                pool.wait_ge(ln_step, MOMENT_STEPS * (b + 1))
                pool.tensor_tensor(rstd[:], var_eps[:], half[:], ALU.pow)\
                    .then_inc(ln_rstd, 1)

            def split_lo(m):
                weight_lo(pool, w_hi_set if m else w0_hi_set, max(m, 1), w_raw[:, m], w_hi[:, m],
                          w_lo[:, m], w_ready[m])

            def y_lo_chunk(j, c):
                pool.wait_ge(y_hi_set, KC * j + c + 1)
                pool.tensor_tensor(y_lo[:, c, :], u[:, c, :], y_hi[:, c, :].bitcast(F32),
                                   ALU.subtract).then_inc(y_lo_set, 1)

            def residual(j, s):
                pool.wait_ge(out_scaled, SUB * j + s + 1)
                pool.wait_ge(res_in[s % 2], 16 * (2 * j + s // 2 + 1))
                pool.tensor_tensor(res[:, s % 2], scaled[:, s % 2], res[:, s % 2], ALU.add)\
                    .then_inc(x2_ready, 1)

            def body(i, before, after):
                lo_piece(i, 1, 0)
                lo_piece(i, 1, 1)
                if before:
                    y_lo_chunk(i - 1, 0)
                    y_lo_chunk(i - 1, 1)
                lo_piece(i, 1, 2)
                if before:
                    y_lo_chunk(i - 1, 2)
                    y_lo_chunk(i - 1, 3)
                lo_piece(i, 1, 3)
                for c in range(KC):
                    lo_piece(i, 2, c)
                if before:
                    for s in range(SUB):
                        residual(i - 1, s)
                if after:
                    layer_norm_rstd(i + 1)
                for m in (3, 4, 5):
                    if not before and m != 4:
                        split_lo(m)
                    for c in range(KC):
                        lo_piece(i, m, c)
                if after:
                    for c in range(KC):
                        lo_piece(i + 1, 0, c)

            pool.memset(half[:], -0.5).then_inc(const_set, 1)
            pool.memset(state[:], 0.0).then_inc(const_set, 1)
            pool.memset(hT[:, :, 0:1], 0.0).then_inc(const_set, 1)
            pool.wait_ge(const_set, 3)
            layer_norm_rstd(0)
            split_lo(0)
            for c in range(KC):
                lo_piece(0, 0, c)
            split_lo(1)
            body(0, False, True)
            with pool.Fori(1, blocks - 1) as i:
                body(i, True, True)
            body(blocks - 1, True, False)
            for c in range(KC):
                y_lo_chunk(blocks - 1, c)
            for s in range(SUB):
                residual(blocks - 1, s)


def feed_forward(nc, x2, out, w1, w2, b1_in, b2, wmod, silu, modulation, identity, batches, seq):
    tokens = x2.shape[0]
    blocks = tokens // TOK
    per_batch = seq // TOK
    x2_view = x2.rearrange("(n p) d -> n p d", p=P)
    out_view = out.rearrange("(n p) d -> n p d", p=P)
    F2_STEPS = JC + SUB - 1
    LN_AT, T_AT, GATE_AT = 5, 9, 7

    with ExitStack() as ctx:
        def sb(name, shape, dt=F32):
            return ctx.enter_context(nc.sbuf_tensor(name, shape, dt))

        def sem(name):
            return ctx.enter_context(nc.semaphore(name))

        w1_hi = sb("w1_hi", [P, KC, INTER], F32R)
        w1_raw = under(nc, "w1_raw", [P, KC, INTER])
        w1_lo = sb("w1_lo", [P, KC, INTER], F32R)
        w2_hi = sb("w2_hi", [P, JC, D], F32R)
        w2_raw = under(nc, "w2_raw", [P, JC, D])
        w2_lo = sb("w2_lo", [P, JC, D], F32R)
        gate = sb("f_gate", [P, batches, D])
        bias = sb("f_bias", [P, D])
        wmod_gate = sb("f_wmod_gate", [P, KC, D])

        w1_view = w1.rearrange("(k p) n -> p k n", p=P)
        w2_view = w2.rearrange("(j p) n -> p j n", p=P)
        parts = []
        for q in range(JC // KC):
            cols, rows = slice(q * D, (q + 1) * D), slice(q * KC, (q + 1) * KC)
            parts += [(w1_view[:, :, cols], w1_raw[:, :, cols], w1_hi[:, :, cols],
                       w1_lo[:, :, cols]),
                      (w2_view[:, rows, :], w2_raw[:, rows, :], w2_hi[:, rows, :],
                       w2_lo[:, rows, :])]

        ident = sb("f_ident", [P, P])
        b1 = sb("b1", [P, JC])
        current = sb("f_current", [P, 2, KC])
        half = sb("f_half", [P, SUB])
        xt = sb("x2t", [P, 2, SUB, D])
        stats = sb("f_stats", [P, SUB, 6])
        mean = sb("f_mean", [P, SUB])
        scratch = sb("f_scratch", [P, 2, SUB])
        var_eps = sb("f_var_eps", [P, SUB])
        rstd = sb("f_rstd", [P, SUB])
        xn = sb("xn", [P, SUB, D])
        hT = sb("h2T", [P, KC, TOK])
        h_hi = sb("h_hi", [P, KC, TOK], F32R)
        h_lo = sb("h_lo", [P, KC, TOK], F32R)
        hid = sb("hid", [P, 2, TOK])
        hid_hi = sb("hid_hi", [P, 2, TOK], F32R)
        hid_lo = sb("hid_lo", [P, 2, TOK], F32R)
        ps = ctx.enter_context(nc.psum_tensor("f_ps", [P, 8, 512], F32))

        w_in = [sem(f"f_w_in{n}") for n in range(len(parts))]
        w0_hi_set = sem("f_w0_hi_set")
        w_hi_set = sem("f_w_hi_set")
        w_ready = [sem(f"f_w_ready{n}") for n in range(len(parts))]
        wmod_in = sem("f_wmod_in")
        gate_done = sem("f_gate_done")
        gate_step = sem("f_gate_step")
        bias_in = sem("f_bias_in")
        current_set = sem("f_current_set")
        const_in = sem("f_const_in")
        half_set = sem("f_half_set")
        x2_in = sem("x2_in")
        stored = sem("stored")
        ln_stats = sem("f_ln_stats")
        ln_step = sem("f_ln_step")
        ln_rstd = sem("f_ln_rstd")
        xn_ready = sem("f_xn_ready")
        t_done = sem("f_t_done")
        h_ready = sem("f_h_ready")
        h_hi_set = sem("h_hi_set")
        h_lo_set = sem("h_lo_set")
        up_done = sem("up_done")
        relu_done = sem("relu_done")
        hid_hi_set = sem("hid_hi_set")
        hid_lo_set = sem("hid_lo_set")
        down_step = sem("down_step")
        sum_biased = sem("sum_biased")
        sum_scaled = sem("sum_scaled")
        out_ready = sem("out_ready")

        def chunk_used(i, j):
            if j < 0:
                j, i = j + JC, i - 1
            return F2_STEPS * i + (j + 1 if j < JC - 1 else F2_STEPS)

        def sum_done(i, s):
            return F2_STEPS * i + JC + s

        up_bank = [ps[:, 0], ps[:, 1]]
        t_bank = [ps[:, 2], ps[:, 3]]
        sums = [ps[:, 4 + s] for s in range(SUB)]

        block = ctx.enter_context(nc.Block())

        @block.sync
        def _(sp):
            sp.dma_start(ident[:], identity).then_inc(const_in, 16)
            sp.dma_start(b1[:], b1_in).then_inc(const_in, 16)

            def load(b):
                wait(sp, stored, 16 * (b - 1))
                wait(sp, xn_ready, SUB * b)
                sp.dma_start(xt[:, b % 2], x2_view[bass.ds(SUB * b, SUB)].rearrange("s p d -> p s d"))\
                  .then_inc(x2_in, 16)

            def store(b):
                sp.wait_ge(out_ready, SUB * (b + 1))
                sp.dma_start(out_view[bass.ds(SUB * b, SUB)].rearrange("s p d -> p s d"), xt[:, b % 2])\
                  .then_inc(stored, 16)

            load(0)
            for n, (source, raw, _, _) in enumerate(parts):
                sp.dma_start(raw, source).then_inc(w_in[n], 16)
                if n == 2:
                    sp.dma_start(wmod_gate[:], wmod.rearrange("(k p) n -> p k n", p=P)[:, :, 5 * D:])\
                      .then_inc(wmod_in, 16)
                    sp.dma_start(bias[:], b2.partition_broadcast(P)).then_inc(bias_in, 16)
            load(1)
            store(0)
            with sp.Fori(1, blocks - 1) as i:
                load(i + 1)
                store(i)
            store(blocks - 1)
            sp.wait_ge(stored, 16 * blocks)

        @block.tensor
        def _(pe):
            def transpose_x(b, s):
                pe.wait_ge(xn_ready, SUB * b + s + 1)
                wait(pe, h_ready, SUB * b + s - 1)
                for c in range(KC):
                    last = pe.transpose(t_bank[s % 2][:, c * P:(c + 1) * P],
                                        xn[:, s, c * P:(c + 1) * P], ident[:])
                last.then_inc(t_done, 1)

            def up(i, j):
                wait(pe, relu_done, JC * i + j - 1)
                cols = slice(j * P, (j + 1) * P)
                if j % KC == 0 and isinstance(i, int) and i == 0:
                    pe.wait_ge(w_ready[j // KC * 2], 1)
                for k in range(KC):
                    if j == 0:
                        pe.wait_ge(h_lo_set, KC * i + k + 1)
                    last = split_product(pe, up_bank[j % 2], w1_hi[:, k, cols], w1_lo[:, k, cols],
                                         h_hi[:, k, :], h_lo[:, k, :], k == 0, k == KC - 1)
                last.then_inc(up_done, 1)

            def down(i, j):
                if j % KC == 0 and isinstance(i, int) and i == 0:
                    pe.wait_ge(w_ready[j // KC * 2 + 1], 1)
                pe.wait_ge(hid_lo_set, JC * i + j + 1)
                for s in range(SUB):
                    if j == 0:
                        wait(pe, sum_biased, SUB * (i - 1) + s + 1)
                    rows = slice(s * P, (s + 1) * P)
                    last = split_product(pe, sums[s], hid_hi[:, j % 2, rows],
                                         hid_lo[:, j % 2, rows], w2_hi[:, j, :], w2_lo[:, j, :],
                                         j == 0, j == JC - 1)
                    if j == JC - 1 or s == SUB - 1:
                        last.then_inc(down_step, 1)

            def body(i, after):
                for j in range(JC):
                    up(i, j)
                    if after and T_AT <= j < T_AT + SUB:
                        transpose_x(i + 1, j - T_AT)
                    if j >= 2:
                        down(i, j - 2)
                    if j == GATE_AT and isinstance(i, int) and i == 0:
                        pe.wait_ge(wmod_in, 16)
                        pe.wait_ge(h_ready, SUB)
                        gate_product(pe, t_bank, wmod_gate, silu, batches, gate_done)
                        pe.wait_ge(gate_step, batches)
                down(i, JC - 2)
                down(i, JC - 1)

            pe.wait_ge(const_in, 32)
            for s in range(SUB):
                transpose_x(0, s)
            body(0, True)
            with pe.Fori(1, blocks - 1) as i:
                body(i, True)
            body(blocks - 1, False)

        @block.scalar
        def _(act):
            def split_hi(n):
                _, raw, hi, _ = parts[n]
                weight_hi(act, w_in[n], raw, hi, w_hi_set)

            def modulated(b, s):
                act.wait_ge(t_done, SUB * b + s + 1)
                if s == 0:
                    act.wait_ge(current_set, b + 1)
                    wait(act, h_lo_set, KC * b)
                for c in range(KC):
                    last = act.activation(
                        hT[:, c, s * P:(s + 1) * P], t_bank[s % 2][:, c * P:(c + 1) * P],
                        ACT.Identity, bias=current[:, 0, c:c + 1],
                        scale=current[:, 1, c:c + 1])
                last.then_inc(h_ready, 1)

            def relu(i, j):
                wait(act, hid_lo_set, JC * i + j - 1)
                act.wait_ge(up_done, JC * i + j + 1)
                act.activation(hid[:, j % 2], up_bank[j % 2], ACT.Relu, bias=b1[:, j:j + 1])\
                   .then_inc(relu_done, 1)

            def body(i, after):
                for j in range(JC):
                    relu(i, j)
                    if after and T_AT <= j < T_AT + SUB:
                        modulated(i + 1, j - T_AT)
                    if isinstance(i, int) and i == 0 and j % KC >= 2 and j < JC - KC:
                        split_hi(j // KC * 2 + j % KC)

            act.wait_ge(const_in, 32)
            for s in range(SUB):
                modulated(0, s)
            split_hi(1)
            body(0, True)
            with act.Fori(1, blocks - 1) as i:
                body(i, True)
            body(blocks - 1, False)

        @block.vector
        def _(dve):
            def layer_norm_stats(b):
                dve.tensor_scalar(current[:], modulation[:, 1, b // per_batch], 1.0, None, ALU.mult)\
                   .then_inc(current_set, 1)
                dve.wait_ge(x2_in, 16 * (b + 1))
                for s in range(SUB):
                    dve.bn_stats(stats[:, s, :], xt[:, b % 2, s, :]).then_inc(ln_stats, 1)
                dve.wait_ge(ln_stats, SUB * (b + 1))
                moments_steps(dve, ln_step, MOMENT_STEPS * b, stats, mean[:], var_eps[:], scratch)

            def layer_norm(b):
                dve.wait_ge(ln_rstd, b + 1)
                wait(dve, t_done, SUB * b)
                for s in range(SUB):
                    dve.tensor_scalar(xn[:, s, :], xt[:, b % 2, s, :], mean[:, s:s + 1],
                                      rstd[:, s:s + 1], ALU.subtract, ALU.mult)\
                       .then_inc(xn_ready, 1)

            def split_h(b):
                dve.wait_ge(h_ready, SUB * (b + 1))
                wait(dve, up_done, JC * b)
                for c in range(KC):
                    dve.tensor_copy(h_hi[:, c, :], hT[:, c, :]).then_inc(h_hi_set, 1)
                    dve.wait_ge(h_hi_set, KC * b + c + 1)
                    dve.tensor_tensor(h_lo[:, c, :], hT[:, c, :], h_hi[:, c, :].bitcast(F32),
                                      ALU.subtract).then_inc(h_lo_set, 1)

            def hidden_hi(i, j):
                dve.wait_ge(relu_done, JC * i + j + 1)
                wait(dve, down_step, chunk_used(i, j - 2) if j >= 2 or not isinstance(i, int)
                     or i > 0 else 0)
                dve.tensor_copy(hid_hi[:, j % 2], hid[:, j % 2]).then_inc(hid_hi_set, 1)

            def sum_out(i, s):
                dve.wait_ge(down_step, sum_done(i, s))
                dve.tensor_tensor(xn[:, s, :], sums[s], bias[:], ALU.add).then_inc(sum_biased, 1)

            def scale_sum(i, s):
                dve.wait_ge(sum_biased, SUB * i + s + 1)
                dve.tensor_tensor(xn[:, s, :], xn[:, s, :], gate[:, i // per_batch, :], ALU.mult)\
                   .then_inc(sum_scaled, 1)
                dve.wait_ge(sum_scaled, SUB * i + s + 1)
                part = xt[:, i % 2, s, :]
                dve.tensor_tensor(part, part, xn[:, s, :], ALU.add).then_inc(out_ready, 1)

            def split_lo(n):
                weight_lo(dve, w_hi_set, n, *parts[n][1:], w_ready[n])

            def body(i, before, after):
                for j in range(JC):
                    hidden_hi(i, j)
                    if before and j < SUB:
                        scale_sum(i - 1, j)
                    if not before and j % KC >= 2 and j < JC - KC:
                        split_lo(j // KC * 2 + j % KC)
                    if not before and j == GATE_AT:
                        dve.wait_ge(gate_done, 1)
                        gate_out(dve, gate[:], wmod_gate[:, 0:batches, :], t_bank, batches,
                                 gate_step)
                        dve.wait_ge(bias_in, 16)
                    if after and j == LN_AT:
                        layer_norm_stats(i + 1)
                    if after and j == LN_AT + 1:
                        layer_norm(i + 1)
                if after:
                    split_h(i + 1)
                for s in range(SUB):
                    sum_out(i, s)

            layer_norm_stats(0)
            layer_norm(0)
            first_weight_hi(dve, w_in[0], parts[0][1], parts[0][2], w0_hi_set)
            split_h(0)
            split_lo(1)
            body(0, False, True)
            with dve.Fori(1, blocks - 1) as i:
                body(i, True, True)
            body(blocks - 1, True, False)
            for s in range(SUB):
                scale_sum(blocks - 1, s)

        @block.gpsimd
        def _(pool):
            def layer_norm_rstd(b):
                pool.wait_ge(ln_step, MOMENT_STEPS * (b + 1))
                pool.tensor_tensor(rstd[:], var_eps[:], half[:], ALU.pow).then_inc(ln_rstd, 1)

            def hidden_lo(i, j):
                pool.wait_ge(hid_hi_set, JC * i + j + 1)
                pool.tensor_tensor(hid_lo[:, j % 2], hid[:, j % 2], hid_hi[:, j % 2].bitcast(F32),
                                   ALU.subtract).then_inc(hid_lo_set, 1)

            def body(i, after):
                for j in range(JC):
                    hidden_lo(i, j)
                    if after and j == LN_AT:
                        layer_norm_rstd(i + 1)

            pool.memset(half[:], -0.5).then_inc(half_set, 1)
            pool.wait_ge(half_set, 1)
            layer_norm_rstd(0)
            weight_lo(pool, w0_hi_set, 1, *parts[0][1:], w_ready[0])
            body(0, True)
            with pool.Fori(1, blocks - 1) as i:
                body(i, True)
            body(blocks - 1, False)


def build(nc, a):
    batches, seq, _ = a["x"].shape
    flat = "b t d -> (b t) d"
    x2 = nc.dram_tensor("x2", (batches * seq, D), F32).ap()
    with ExitStack() as ctx:
        silu = ctx.enter_context(nc.sbuf_tensor("silu", [P, KC, batches], F32))
        modulation = ctx.enter_context(nc.sbuf_tensor("modulation", [P, 2, batches, 2, KC], F32))
        attention(nc, a["x"].rearrange(flat), x2, a["mix"], [a[f"W_{m}"] for m in PROJ],
                  a["W_out"], a["b_out"], a["gn"], a["cT"], a["wmod"], silu, modulation,
                  a["identity"], a["centering"], a["group_mean"], a["keep"], batches, seq)
        feed_forward(nc, x2, a["out"].rearrange(flat), a["W1"], a["W2"], a["b1"], a["b2"],
                     a["wmod"], silu, modulation, a["identity"], batches, seq)


def kernel(**inputs):
    import numpy as np
    import concourse.bacc as bacc
    from concourse.bass_utils import run_bass_kernel_spmd

    def attn(name):
        return np.asarray(inputs[f"L0_attn_{name}"])

    def by_chunk(vector):
        return vector.reshape(-1, P).T

    x = attn("x")
    batches, seq, _ = x.shape
    arrays = {"x": x, "W1": inputs["L0_ffn_W1"], "W2": inputs["L0_ffn_W2"],
              "wmod": inputs["L0_wmod"], "W_out": attn("W_out").T}
    for m in PROJ:
        arrays[f"W_{m}"] = attn(f"W_{m}").T
    arrays["mix"] = np.concatenate([by_chunk(attn(f"x_{m}").reshape(D)) for m in PROJ], axis=1)
    arrays["gn"] = np.stack([by_chunk(attn("gn_w")), by_chunk(attn("gn_b"))], axis=1)
    arrays["cT"] = np.asarray(inputs["L0_c"]).T.reshape(KC, P, batches).transpose(1, 0, 2)
    arrays["b_out"] = attn("b_out").reshape(1, D)
    arrays["b1"] = by_chunk(np.asarray(inputs["L0_ffn_b1"]))
    arrays["b2"] = np.asarray(inputs["L0_ffn_b2"]).reshape(1, D)
    same = np.kron(np.eye(GPC), np.full((GROUP, GROUP), 1.0 / GROUP))
    keep = np.ones((P, batches * seq // TOK + 1))
    keep[:, ::seq // TOK] = 0.0
    arrays["identity"] = np.eye(P)
    arrays["centering"] = np.eye(P) - same
    arrays["group_mean"] = same[:, ::GROUP]
    arrays["keep"] = keep
    arrays = {n: np.ascontiguousarray(v, np.float32) for n, v in arrays.items()}

    nc = bacc.Bacc("TRN2", target_bir_lowering=False, num_devices=1)
    aps = {n: nc.dram_tensor(f"in_{n}", v.shape, F32, kind="ExternalInput").ap()
           for n, v in arrays.items()}
    aps["out"] = nc.dram_tensor("out", x.shape, F32, kind="ExternalOutput").ap()
    build(nc, aps)
    result = run_bass_kernel_spmd(nc, [{f"in_{n}": v for n, v in arrays.items()}], core_ids=[0])
    return result.results[0]["out"]
```

```python
from contextlib import ExitStack

import concourse.bass as bass
from concourse import mybir
from concourse.alu_op_type import AluOpType as ALU

F32 = mybir.dt.float32
F32R = mybir.dt.float32r
I32 = mybir.dt.int32
ACT = mybir.ActivationFunctionType

P = 128
D = 512
KC = D // P
TOK = 512
SUB = TOK // P
HEADS = 16
GROUP = D // HEADS
GPC = P // GROUP
INTER = 2048
JC = INTER // P
LN_EPS = 1e-5
GN_EPS = 0.00064
GATE_MIN = 0.25

PROJ = ["k", "a", "v", "w", "r", "g"]
NP = len(PROJ)
PIECES = NP * KC
HI_RING = 4
F32_RING = 3
GATE_RING = 3
PROJ_BANKS = 6
AUX = [6, 7]
STEPS = 2 * KC - 1


def wait(engine, semaphore, value):
    if not isinstance(value, int) or value > 0:
        engine.wait_ge(semaphore, value)


def split_product(pe, acc, a_hi, a_lo, b_hi, b_lo, first, last):
    pe.matmul(acc, a_hi, b_hi, start=first, stop=False)
    pe.matmul(acc, a_hi, b_lo, start=False, stop=False)
    return pe.matmul(acc, a_lo, b_hi, start=False, stop=last)


def moments_steps(dve, step, steps_before, stats, mean, var_eps, scratch):
    mean_e, mean_o, m2_e, m2_o = (stats[:, :, q] for q in (1, 4, 2, 5))
    diff, m2 = scratch[:, 0, :], scratch[:, 1, :]
    dve.tensor_tensor(diff, mean_e, mean_o, ALU.subtract).then_inc(step, 1)
    dve.scalar_tensor_tensor(m2, m2_e, D * LN_EPS, m2_o, ALU.add, ALU.add).then_inc(step, 1)
    dve.tensor_tensor(mean, mean_e, mean_o, ALU.add).then_inc(step, 1)
    dve.wait_ge(step, steps_before + 3)
    dve.scalar_tensor_tensor(diff, diff, 0.25, diff, ALU.mult, ALU.mult).then_inc(step, 1)
    dve.tensor_scalar(mean, mean, 0.5, None, ALU.mult).then_inc(step, 1)
    dve.wait_ge(step, steps_before + 5)
    dve.scalar_tensor_tensor(var_eps, m2, 1.0 / D, diff, ALU.mult, ALU.add).then_inc(step, 1)


MOMENT_STEPS = 6


def inverse_root(dve, step, steps_before, value, root, bits, scratch):
    count = [steps_before]

    def then(instruction):
        instruction.then_inc(step, 1)
        count[0] += 1
        dve.wait_ge(step, count[0])

    then(dve.tensor_scalar(bits, value.bitcast(I32), 1, None, ALU.logical_shift_right))
    then(dve.tensor_scalar(bits, bits, -1.0, float(0x5F3759DF), ALU.mult, ALU.add))
    for _ in range(NEWTON):
        then(dve.tensor_tensor(scratch, root, root, ALU.mult))
        then(dve.scalar_tensor_tensor(scratch, scratch, -0.5, value, ALU.mult, ALU.mult))
        then(dve.scalar_tensor_tensor(root, scratch, 1.5, root, ALU.add, ALU.mult))


NEWTON = 3
ROOT_STEPS = 2 + 3 * NEWTON


def under(nc, name, shape):
    with nc.sbuf_tensor(name, shape, F32) as tile:
        return tile


def weight_hi(act, arrived, raw, tile_hi, hi_set):
    act.wait_ge(arrived, 16)
    act.activation(tile_hi, raw, ACT.Copy).then_inc(hi_set, 1)


def weight_lo(engine, hi_set, count, raw, tile_hi, tile_lo, ready):
    engine.wait_ge(hi_set, count)
    engine.tensor_tensor(tile_lo, raw, tile_hi.bitcast(F32), ALU.subtract)\
          .then_inc(ready, 1)


def modulation_rows(pe, rows, wmod_group, silu, done):
    for k in range(KC):
        last = pe.matmul(rows, silu[:, k, :], wmod_group[:, k, :], start=k == 0, stop=k == KC - 1)
    last.then_inc(done, 1)


def modulation_columns(pe, columns, rows, ident, batches, done):
    for q in range(2):
        for c in range(KC):
            at = (q * KC + c) * batches
            last = pe.transpose(columns[:, at:at + batches], rows[:, q, c * P:(c + 1) * P],
                                ident[0:batches, 0:batches])
    last.then_inc(done, 1)


def modulation_out(dve, target, columns, batches, done):
    for q in range(2):
        got = columns[:, q * KC * batches:(q + 1) * KC * batches]\
            .rearrange("p (c b) -> p c b", b=batches)
        for b in range(batches):
            last = dve.tensor_scalar(target[:, b, q, :], got[:, :, b], float(q), None, ALU.add)
    last.then_inc(done, 1)


def gate_product(pe, rows, wmod_group, silu, batches, done):
    for b in range(batches):
        for k in range(KC):
            last = pe.matmul(rows[b], silu[:, k, b:b + 1].broadcast_to([P, P]),
                             wmod_group[:, k, :], start=k == 0, stop=k == KC - 1)
    last.then_inc(done, 1)


def gate_out(dve, gate, raw, rows, batches, step):
    for b in range(batches):
        dve.tensor_copy(raw[:, b, :], rows[b]).then_inc(step, 1)
    dve.wait_ge(step, batches)
    dve.scalar_tensor_tensor(gate, raw, -1.0, raw, ALU.mult, ALU.max).then_inc(step, 1)
    dve.wait_ge(step, batches + 1)
    dve.tensor_scalar(gate, gate, GATE_MIN, None, ALU.max).then_inc(step, 1)
    dve.wait_ge(step, batches + 2)
    dve.scalar_tensor_tensor(raw, raw, 0.0, gate, ALU.is_ge, ALU.mult).then_inc(step, 1)
    dve.wait_ge(step, batches + 3)
    dve.scalar_tensor_tensor(gate, raw, 2.0, gate, ALU.mult, ALU.subtract).then_inc(step, 1)
    dve.wait_ge(step, batches + 4)


def attention(nc, x, x2, mixes, w_proj, w_out, b_out, gn, cT_in, wmod, w1_view, silu, modulation,
              hT, w1_raw, identity, centering, group_mean, keep_in, batches, seq):
    tokens = x.shape[0]
    blocks = tokens // TOK
    per_batch = seq // TOK
    x_view = x.rearrange("(n p) d -> n p d", p=P)
    x2_view = x2.rearrange("(n p) d -> n p d", p=P)

    with ExitStack() as ctx:
        def sb(name, shape, dt=F32):
            return ctx.enter_context(nc.sbuf_tensor(name, shape, dt))

        def sem(name):
            return ctx.enter_context(nc.semaphore(name))

        w_hi = sb("w_hi", [P, NP + 1, KC, D], F32R)
        w_raw = under(nc, "w_raw", [P, NP + 1, KC, D])
        w_lo = sb("w_lo", [P, NP + 1, KC, D], F32R)
        gate = sb("gate", [P, batches, D])
        bias = sb("bias", [P, D])
        cT = sb("cT", [P, KC, batches])
        sig = sb("sig", [P, KC, batches])

        ident = sb("ident", [P, P])
        center_in = sb("center_in", [P, P])
        center = sb("center", [P, P], F32R)
        g_mean = sb("g_mean", [P, GPC])
        mix = sb("mix", [P, PIECES])
        unmix = sb("unmix", [P, PIECES])
        gn_wb = sb("gn_wb", [P, 2, KC])
        keep = sb("keep", [P, blocks + 1])
        current = sb("current", [P, 2, KC])
        keep_now = sb("keep_now", [P, 1])
        half = sb("half", [P, SUB])
        state = sb("state", [P, KC])

        xt = sb("xt", [P, SUB, D])
        stats = sb("stats", [P, SUB, 6])
        mean = sb("mean", [P, SUB])
        scratch = sb("scratch", [P, 2, SUB])
        var_eps = sb("var_eps", [P, SUB])
        rstd = sb("rstd", [P, SUB])
        mixed_in = sb("mixed_in", [P, F32_RING, TOK])
        in_hi = sb("in_hi", [P, HI_RING, TOK], F32R)
        in_lo = sb("in_lo", [P, HI_RING, TOK], F32R)
        u = sb("u", [P, KC, TOK])
        gates = sb("gates", [P, GATE_RING, TOK])
        g_sig = sb("g_sig", [P, KC, TOK])
        square = rstd_wide = scaled = sb("square_wide_scaled", [P, 2, TOK])
        g_var = sb("g_var", [P, SUB * HEADS])
        g_rstd = sb("g_rstd", [P, SUB * HEADS])
        g_scratch = sb("g_scratch", [P, SUB * HEADS])
        wmod_y = under(nc, "wmod_y", [P, 2, KC, D])
        y_hi = sb("y_hi", [P, KC, TOK], F32R)
        y_lo = sb("y_lo", [P, KC, TOK], F32R)
        wmod_tile = {"scale": wmod_y[:, 0], "shift": wmod_y[:, 1], "gate": g_sig[:]}
        res = sb("res", [P, 2, D])
        ps = ctx.enter_context(nc.psum_tensor("ps", [P, 8, 512], F32))

        c_in = sem("c_in")
        sig_ready = sem("sig_ready")
        silu_ready = sem("silu_ready")
        wmod_in = {q: sem(f"wmod_in_{q}") for q in wmod_tile}
        mod_done = sem("mod_done")
        mod_rows_set = sem("mod_rows_set")
        mod_set = sem("mod_set")
        gate_step = sem("gate_step")
        bias_in = sem("bias_in")
        w_in = [sem(f"w_in{m}") for m in range(NP + 1)]
        w0_hi_set = sem("w0_hi_set")
        w_hi_set = sem("w_hi_set")
        w_ready = [sem(f"w_ready{m}") for m in range(NP + 1)]
        w1_in = sem("w1_in")
        last_ready = sem("last_ready")
        last_out = [sem(f"last_out{s}") for s in range(SUB)]
        current_set = sem("current_set")
        const_in = sem("const_in")
        const_set = sem("const_set")
        unmix_set = sem("unmix_set")
        x_in = sem("x_in")
        ln_stats = sem("ln_stats")
        ln_step = sem("ln_step")
        ln_rstd = sem("ln_rstd")
        xn_ready = sem("xn_ready")
        t_done = sem("t_done")
        h_ready = sem("h_ready")
        carried = sem("carried")
        prev_scaled = sem("prev_scaled")
        mix_ready = sem("mix_ready")
        hi_ready = sem("hi_ready")
        lo_ready = sem("lo_ready")
        proj_step = sem("proj_step")
        act_out = sem("act_out")
        v_out = sem("v_out")
        gate_used = sem("gate_used")
        state_kept = sem("state_kept")
        rs_hi_set = sem("rs_hi_set")
        rs_lo_set = sem("rs_lo_set")
        center_done = sem("center_done")
        centered = sem("centered")
        squared = sem("squared")
        var_done = sem("var_done")
        g_var_set = sem("g_var_set")
        root_step = sem("root_step")
        wide_set = sem("wide_set")
        wide_done = sem("wide_done")
        normed = sem("normed")
        gated = sem("gated")
        y_hi_set = sem("y_hi_set")
        y_lo_set = sem("y_lo_set")
        out_done = sem("out_done")
        out_biased = sem("out_biased")
        out_scaled = sem("out_scaled")
        res_in = [sem(f"res_in{s}") for s in range(2)]
        x2_ready = sem("x2_ready")
        x2_out = [sem(f"x2_out{s}") for s in range(2)]

        def aux(n):
            return ps[:, AUX[n % 2]]

        def proj_bank(n):
            return ps[:, n % PROJ_BANKS]

        def input_used(i, n):
            if n < 0:
                n, i = n + PIECES, i - 1
            m, k = divmod(n, KC)
            return STEPS * NP * i + STEPS * m + (k + 1 if k < KC - 1 else STEPS)

        def output_done(i, m, o):
            return STEPS * NP * i + STEPS * m + KC + o

        mod_rows = [aux(q)[0:batches] for q in range(2)]
        mod_rows_sb = square[0:batches]
        mod_columns = aux(0)

        w_view = [w.rearrange("(k p) n -> p k n", p=P) for w in (*w_proj, w_out)]
        wmod_view = wmod.rearrange("(k p) n -> p k n", p=P)
        gate_rows = [aux(b) for b in range(batches)]
        block = ctx.enter_context(nc.Block())

        @block.sync
        def _(sp):
            def load_wmod(name, q):
                sp.dma_start(wmod_tile[name], wmod_view[:, :, q * D:(q + 1) * D])\
                  .then_inc(wmod_in[name], 16)

            def load_weight(m):
                sp.dma_start(w_raw[:, m], w_view[m]).then_inc(w_in[m], 16)

            sp.dma_start(cT[:], cT_in).then_inc(c_in, 16)
            load_wmod("scale", 1)
            load_wmod("shift", 0)
            loads = [(ident, identity), (center_in, centering), (g_mean, group_mean),
                     (mix, mixes), (gn_wb, gn), (keep, keep_in)]
            for tile, source in loads:
                sp.dma_start(tile[:], source).then_inc(const_in, 16)

            def load_x(b, view=x_view, at=None):
                wait(sp, t_done, KC * b)
                rows = bass.ds(SUB * (b if at is None else at), SUB)
                sp.dma_start(xt[:], view[rows].rearrange("s p d -> p s d")).then_inc(x_in, 16)

            def residual(j):
                def load(s):
                    wait(sp, x2_out[s % 2], 16 * (2 * j + s // 2))
                    sp.dma_start(res[:, s % 2], x_view[SUB * j + s]).then_inc(res_in[s % 2], 16)

                def store(s):
                    sp.wait_ge(x2_ready, SUB * j + s + 1)
                    sp.dma_start(x2_view[SUB * j + s], res[:, s % 2]).then_inc(x2_out[s % 2], 16)

                load(0)
                load(1)
                for s in range(2, SUB):
                    store(s - 2)
                    load(s)
                store(SUB - 2)
                store(SUB - 1)

            def body(i):
                load_x(i + 1)
                residual(i - 1)

            load_x(0)
            sp.dma_start(bias[:], b_out.partition_broadcast(P)).then_inc(bias_in, 16)
            load_weight(0)
            load_weight(1)
            load_wmod("gate", 2)
            load_weight(2)
            load_weight(3)
            load_x(1)
            load_weight(4)
            load_weight(5)
            sp.wait_ge(mod_done, 2)
            load_wmod("scale", 4)
            load_wmod("shift", 3)
            load_weight(NP)
            body(1)
            with sp.Fori(2, blocks - 1) as i:
                body(i)
            for s in range(2):
                sp.wait_ge(x2_out[s], 16 * 2)
            load_x(blocks, x2_view, 0)
            residual(blocks - 2)
            load_x(blocks + 1, x_view, blocks - 1)
            sp.wait_ge(proj_step, STEPS * NP * blocks)
            sp.dma_start(w1_raw[:], w1_view).then_inc(w1_in, 16)
            for s in range(SUB):
                sp.wait_ge(last_ready, s + 1)
                sp.dma_start(x2_view[SUB * (blocks - 1) + s], xt[:, s]).then_inc(last_out[s], 16)
            for s in range(SUB):
                sp.wait_ge(last_out[s], 16)
            sp.wait_ge(w1_in, 16)
            for s in range(2):
                sp.wait_ge(x2_out[s], 16 * 2 * (blocks - 1))

        @block.tensor
        def _(pe):
            def bank_free(i, n):
                n -= PROJ_BANKS
                if n < 0:
                    n, i = n + PIECES, i - 1
                m, o = divmod(n, KC)
                if PROJ[m] == "v":
                    wait(pe, v_out, KC * i + o + 1)
                else:
                    wait(pe, act_out, (PIECES - KC) * i + n + 1 - (KC if m > 2 else 0))

            def modulate(phase):
                for name, rows in (("scale", mod_rows[1]), ("shift", mod_rows[0])):
                    pe.wait_ge(wmod_in[name], 16 * (phase + 1))
                    modulation_rows(pe, rows, wmod_tile[name], silu, mod_done)

            def turn_modulation(phase):
                pe.wait_ge(mod_rows_set, 2 * (phase + 1))
                modulation_columns(pe, mod_columns, mod_rows_sb, ident, batches, mod_done)

            def project(i, m, k, between={}):
                n = m * KC + k
                slot = n % HI_RING
                if isinstance(i, int) and i == 0 and m == 0:
                    pe.wait_ge(w_ready[m], k + 1)
                elif k == 0 and isinstance(i, int) and i == 0:
                    pe.wait_ge(w_ready[m], 1)
                pe.wait_ge(lo_ready, PIECES * i + n + 1)
                for o in range(KC):
                    if k == 0:
                        bank_free(i, m * KC + o)
                    cols = slice(o * P, (o + 1) * P)
                    last = split_product(pe, proj_bank(m * KC + o), w_hi[:, m, k, cols],
                                         w_lo[:, m, k, cols], in_hi[:, slot], in_lo[:, slot],
                                         k == 0, k == KC - 1)
                    if k == KC - 1 or o == KC - 1:
                        last.then_inc(proj_step, 1)
                    if o in between:
                        between[o]()

            def transpose_x(b, chunks):
                for c in chunks:
                    if c == 0:
                        pe.wait_ge(xn_ready, SUB * (b + 1))
                    if c < 2 and isinstance(b, int) and b < 2:
                        wait(pe, h_ready, KC * (b - 1) + c + 3)
                    elif c < 2:
                        pe.wait_ge(out_biased, SUB * (b - 2) + c + 3)
                    else:
                        pe.wait_ge(h_ready, KC * b + c - 1)
                    for s in range(SUB):
                        last = pe.transpose(aux(c + 1)[:, s * P:(s + 1) * P],
                                            xt[:, s, c * P:(c + 1) * P], ident[:])
                    last.then_inc(t_done, 1)

            def center_chunk(i, c):
                pe.wait_ge(rs_lo_set, KC * i + c + 1)
                if c >= 2:
                    pe.wait_ge(centered, KC * i + c - 1)
                else:
                    pe.wait_ge(h_ready, KC * (i + 1) + c + 3)
                pe.matmul(aux(c + 1), center[:], y_hi[:, c, :], start=True, stop=False)
                pe.matmul(aux(c + 1), center[:], y_lo[:, c, :], start=False, stop=True)\
                  .then_inc(center_done, 1)

            def variance(i, c):
                pe.wait_ge(squared, KC * i + c + 1)
                if c == 0:
                    pe.wait_ge(centered, KC * i + KC)
                for s in range(SUB):
                    at = s * HEADS + c * GPC
                    last = pe.matmul(aux(0)[:, at:at + GPC], square[:, c % 2, s * P:(s + 1) * P],
                                     g_mean[:], start=True, stop=True)
                last.then_inc(var_done, 1)

            def widen(j, s):
                pe.wait_ge(wide_set, SUB * j + s + 1)
                if s == 1:
                    pe.wait_ge(g_var_set, j + 1)
                if s >= 2:
                    pe.wait_ge(normed, SUB * j + s - 1)
                for c in range(KC):
                    last = pe.transpose(aux(s + 1)[:, c * P:(c + 1) * P],
                                        rstd_wide[:, s % 2, c * P:(c + 1) * P], ident[:])
                last.then_inc(wide_done, 1)

            def output(j):
                for s in range(SUB):
                    if s < 2:
                        pe.wait_ge(normed, SUB * j + s + 3)
                    else:
                        pe.wait_ge(out_biased, SUB * j + s - 1)
                    for k in range(KC):
                        if s == 0:
                            pe.wait_ge(y_lo_set, KC * j + k + 1)
                        rows = slice(s * P, (s + 1) * P)
                        last = split_product(pe, aux(s + 1), y_hi[:, k, rows], y_lo[:, k, rows],
                                             w_hi[:, NP, k, :], w_lo[:, NP, k, :],
                                             k == 0, k == KC - 1)
                    last.then_inc(out_done, 1)

            def body(i, before):
                first = not before
                project(i, 0, 0)
                project(i, 0, 1)
                if before:
                    widen(i - 1, 0)
                    widen(i - 1, 1)
                    project(i, 0, 2, between={1: lambda: widen(i - 1, 2),
                                              3: lambda: widen(i - 1, 3)})
                else:
                    project(i, 0, 2)
                project(i, 0, 3)
                for k in range(KC):
                    project(i, 1, k)
                if before:
                    output(i - 1)
                if first:
                    pe.wait_ge(wmod_in["gate"], 16)
                    pe.wait_ge(h_ready, KC)
                    gate_product(pe, gate_rows, wmod_tile["gate"], silu, batches, mod_done)
                for m in (2, 3, 4):
                    for k in range(KC):
                        project(i, m, k)
                        if first and (m, k) == (4, 0):
                            turn_modulation(1)
                        if first and (m, k) == (4, KC - 2):
                            pe.wait_ge(mod_set, 2)
                        if (m, k) == (4, KC - 2):
                            transpose_x(i + 1, (0, 1))
                    if first and m == 3:
                        pe.wait_ge(gate_step, batches)
                        modulate(1)
                transpose_x(i + 1, (2, 3))
                project(i, 5, 0)
                center_chunk(i, 0)
                project(i, 5, 1, between={1: lambda: center_chunk(i, 1)})
                center_chunk(i, 2)
                project(i, 5, 2, between={0: lambda: center_chunk(i, 3)})
                variance(i, 0)
                project(i, 5, 3, between={0: lambda: variance(i, 1), 2: lambda: variance(i, 2)})
                variance(i, 3)

            pe.wait_ge(silu_ready, 1)
            modulate(0)
            pe.wait_ge(const_in, 6 * 16)
            turn_modulation(0)
            pe.wait_ge(mod_set, 1)
            transpose_x(0, range(KC))
            body(0, False)
            with pe.Fori(1, blocks - 1) as i:
                body(i, True)
            body(blocks - 1, True)
            for s in range(SUB):
                widen(blocks - 1, s)
            output(blocks - 1)

        @block.scalar
        def _(act):
            def scale_prev(b, m, c):
                n = m * KC + c
                if n < KC:
                    act.wait_ge(h_ready, KC * b + c + 1)
                if n == 0:
                    wait(act, carried, b)
                wait(act, lo_ready, PIECES * b + n + 1 - F32_RING)
                act.activation(mixed_in[:, n % F32_RING], hT[:, c, 0:TOK], ACT.Copy,
                               scale=mix[:, n:n + 1]).then_inc(prev_scaled, 1)

            def out_of_psum(i, m):
                name = PROJ[m]
                func = ACT.Tanh if name == "k" else ACT.Sigmoid
                for o in range(KC):
                    if name == "k":
                        wait(act, gated, KC * (i - 1) + o + 1)
                        target = u[:, o, :]
                    elif name == "g":
                        wait(act, y_lo_set, KC * (i - 1) + o + 1)
                        target = g_sig[:, o, :]
                    else:
                        n = {"a": 0, "w": 1, "r": 2}[name] * KC + o
                        wait(act, gate_used, 3 * KC * i + n + 1 - GATE_RING)
                        target = gates[:, n % GATE_RING]
                    act.wait_ge(proj_step, output_done(i, m, o))
                    act.activation(target, proj_bank(m * KC + o), func,
                                   scale=-1.0 if name == "w" else 1.0).then_inc(act_out, 1)

            def split_hi(m):
                weight_hi(act, w_in[m], w_raw[:, m], w_hi[:, m], w_hi_set)

            def rows_out(phase):
                for n, q in enumerate((1, 0)):
                    act.wait_ge(mod_done, (1, 5)[phase] + n)
                    act.activation(mod_rows_sb[:, q, :], mod_rows[q], ACT.Copy)\
                       .then_inc(mod_rows_set, 1)

            def modulated(b, chunks):
                act.wait_ge(current_set, b + 1)
                wait(act, mix_ready, PIECES * b)
                if 0 in chunks and not (isinstance(b, int) and b == 0):
                    act.activation(hT[:, :, 0:1], hT[:, :, TOK:TOK + 1], ACT.Copy,
                                   scale=keep_now[:]).then_inc(carried, 1)
                for c in chunks:
                    if c == 0:
                        wait(act, carried, b)
                    act.wait_ge(t_done, KC * b + c + 1)
                    act.activation(hT[:, c, 1:], aux(c + 1), ACT.Identity,
                                   bias=current[:, 0, c:c + 1], scale=current[:, 1, c:c + 1])\
                       .then_inc(h_ready, 1)

            def center_out(i, c):
                act.wait_ge(center_done, KC * i + c + 1)
                act.activation(u[:, c, :], aux(c + 1), ACT.Copy).then_inc(centered, 1)

            def square_chunk(i, c):
                act.wait_ge(centered, KC * i + c + 1)
                if c >= 2:
                    act.wait_ge(var_done, KC * i + c - 1)
                act.activation(square[:, c % 2], u[:, c, :], ACT.Square).then_inc(squared, 1)

            def body(i, before, after):
                for c in range(KC):
                    scale_prev(i, 1, c)
                out_of_psum(i, 0)
                for m in range(1, NP - 1):
                    if not before:
                        split_hi(m + 1)
                    for c in range(KC):
                        scale_prev(i, m + 1, c)
                    if PROJ[m] == "r":
                        modulated(i + 1, (0, 1))
                    if PROJ[m] != "v":
                        out_of_psum(i, m)
                    if not before and PROJ[m] == "w":
                        rows_out(1)
                modulated(i + 1, (2, 3))
                for c in range(KC):
                    if after and c < KC - 1:
                        scale_prev(i + 1, 0, c)
                    center_out(i, c)
                    if c == 1:
                        square_chunk(i, 0)
                        square_chunk(i, 1)
                if after:
                    scale_prev(i + 1, 0, KC - 1)
                square_chunk(i, 2)
                square_chunk(i, 3)
                out_of_psum(i, NP - 1)
                if not before:
                    split_hi(NP)

            act.wait_ge(c_in, 16)
            act.activation(sig[:], cT[:], ACT.Sigmoid).then_inc(sig_ready, 1)
            rows_out(0)
            act.wait_ge(const_in, 6 * 16)
            act.wait_ge(const_set, 3)
            for c in range(KC):
                modulated(0, (c,))
                if c < F32_RING:
                    scale_prev(0, 0, c)
            split_hi(1)
            scale_prev(0, 0, KC - 1)
            body(0, False, True)
            with act.Fori(1, blocks - 1) as i:
                body(i, True, True)
            body(blocks - 1, True, False)

        @block.vector
        def _(dve):
            def split_lo(m):
                weight_lo(dve, w_hi_set, m, w_raw[:, m], w_hi[:, m], w_lo[:, m], w_ready[m])

            def take_modulation(phase):
                dve.wait_ge(mod_done, (3, 7)[phase])
                modulation_out(dve, modulation[:, phase], mod_columns, batches, mod_set)
                dve.wait_ge(mod_set, phase + 1)

            def set_current(b):
                dve.tensor_scalar(keep_now[:], keep[:, bass.ds(b, 1)], 1.0, None, ALU.mult)
                source = modulation[:, 1, 0] if isinstance(b, int) and b == blocks \
                    else modulation[:, 0, b // per_batch]
                dve.tensor_scalar(current[:], source, 1.0, None, ALU.mult)\
                   .then_inc(current_set, 1)

            def layer_norm_stats(b, s):
                dve.wait_ge(x_in, 16 * (b + 1))
                dve.bn_stats(stats[:, s, :], xt[:, s, :]).then_inc(ln_stats, 1)

            def layer_norm_moments(b):
                dve.wait_ge(ln_stats, SUB * (b + 1))
                moments_steps(dve, ln_step, MOMENT_STEPS * b, stats, mean[:], var_eps[:], scratch)

            def layer_norm(b):
                dve.wait_ge(ln_rstd, b + 1)
                for s in range(SUB):
                    dve.tensor_scalar(xt[:, s, :], xt[:, s, :], mean[:, s:s + 1],
                                      rstd[:, s:s + 1], ALU.subtract, ALU.mult)\
                       .then_inc(xn_ready, 1)

            def mix_piece(b, m, c):
                n = m * KC + c
                made = mixed_in[:, n % F32_RING]
                dve.wait_ge(prev_scaled, PIECES * b + n + 1)
                dve.scalar_tensor_tensor(made, hT[:, c, 1:1 + TOK], unmix[:, n:n + 1], made,
                                         ALU.mult, ALU.add).then_inc(mix_ready, 1)

            def hi_piece(b, m, c):
                n = m * KC + c
                dve.wait_ge(mix_ready, PIECES * b + n + 1)
                wait(dve, proj_step, input_used(b, n - HI_RING) if n >= HI_RING or
                     not isinstance(b, int) or b > 0 else 0)
                dve.tensor_copy(in_hi[:, n % HI_RING], mixed_in[:, n % F32_RING])\
                   .then_inc(hi_ready, 1)

            def input_and_use(i, m, use):
                mix_piece(i, m, 0)
                hi_piece(i, m, 0)
                mix_piece(i, m, 1)
                hi_piece(i, m, 1)
                mix_piece(i, m, 2)
                mix_piece(i, m, 3)
                hi_piece(i, m, 2)
                use(i, 0)
                use(i, 1)
                hi_piece(i, m, 3)
                use(i, 2)
                use(i, 3)

            def use_a(i, c):
                dve.wait_ge(act_out, 5 * KC * i + KC + c + 1)
                dve.tensor_tensor(u[:, c, :], u[:, c, :], gates[:, c % GATE_RING], ALU.mult)\
                   .then_inc(gate_used, 1)

            def use_v(i, c):
                dve.wait_ge(proj_step, output_done(i, 2, c))
                dve.wait_ge(gate_used, 3 * KC * i + c + 1)
                dve.tensor_tensor(u[:, c, :], u[:, c, :], proj_bank(2 * KC + c), ALU.mult)\
                   .then_inc(v_out, 1)

            def scan(i, c):
                dve.wait_ge(act_out, 5 * KC * i + 2 * KC + c + 1)
                dve.wait_ge(v_out, KC * i + c + 1)
                wait(dve, state_kept, KC * (i - 1) + c + 1)
                dve.tensor_tensor_scan(u[:, c, :], gates[:, (KC + c) % GATE_RING], u[:, c, :],
                                       state[:, c:c + 1], ALU.mult, ALU.add)\
                   .then_inc(gate_used, 1)
                dve.wait_ge(gate_used, 3 * KC * i + KC + c + 1)
                dve.tensor_scalar(state[:, c:c + 1], u[:, c, TOK - 1:TOK],
                                  keep[:, bass.ds(i + 1, 1)], None, ALU.mult)\
                   .then_inc(state_kept, 1)

            def use_r(i, c):
                dve.wait_ge(act_out, 5 * KC * i + 3 * KC + c + 1)
                dve.wait_ge(state_kept, KC * i + c + 1)
                dve.tensor_tensor(u[:, c, :], u[:, c, :], gates[:, (2 * KC + c) % GATE_RING],
                                  ALU.mult).then_inc(gate_used, 1)
                dve.wait_ge(gate_used, 3 * KC * i + 2 * KC + c + 1)
                if c == 0:
                    wait(dve, out_done, SUB * i)
                dve.tensor_copy(y_hi[:, c, :], u[:, c, :]).then_inc(rs_hi_set, 1)
                dve.wait_ge(rs_hi_set, KC * i + c + 1)
                dve.tensor_tensor(y_lo[:, c, :], u[:, c, :], y_hi[:, c, :].bitcast(F32),
                                  ALU.subtract).then_inc(rs_lo_set, 1)

            def group_variance(j):
                dve.wait_ge(var_done, KC * (j + 1))
                dve.tensor_scalar(g_var[:], aux(0)[:, 0:SUB * HEADS], GN_EPS, None, ALU.add)\
                   .then_inc(g_var_set, 1)
                dve.wait_ge(g_var_set, j + 1)
                inverse_root(dve, root_step, ROOT_STEPS * j, g_var[:], g_rstd[:],
                             g_rstd[:].bitcast(I32), g_scratch[:])

            def wide(j, s):
                if s >= 2:
                    dve.wait_ge(wide_done, SUB * j + s - 1)
                dve.tensor_copy(
                    rstd_wide[:, s % 2].rearrange("p (g c) -> p g c", c=GROUP),
                    g_rstd[:, s * HEADS:(s + 1) * HEADS].unsqueeze(2)
                    .broadcast_to([P, HEADS, GROUP])).then_inc(wide_set, 1)

            def normalise(j, s):
                dve.wait_ge(wide_done, SUB * j + s + 1)
                for c in range(KC):
                    part = u[:, c, s * P:(s + 1) * P]
                    last = dve.scalar_tensor_tensor(part, aux(s + 1)[:, c * P:(c + 1) * P],
                                                    gn_wb[:, 0, c:c + 1], part, ALU.mult, ALU.mult)
                last.then_inc(normed, 1)

            def gate_y(j, c):
                dve.wait_ge(normed, SUB * (j + 1))
                dve.wait_ge(act_out, 5 * KC * j + 4 * KC + c + 1)
                dve.scalar_tensor_tensor(g_sig[:, c, :], u[:, c, :], gn_wb[:, 1, c:c + 1],
                                         g_sig[:, c, :], ALU.add, ALU.mult).then_inc(gated, 1)
                dve.wait_ge(gated, KC * j + c + 1)
                dve.tensor_copy(y_hi[:, c, :], g_sig[:, c, :]).then_inc(y_hi_set, 1)

            def scale_output(j, s):
                slot = scaled[:, s % 2]
                dve.wait_ge(out_done, SUB * j + s + 1)
                if s >= 2 and isinstance(j, int) and j == blocks - 1:
                    dve.wait_ge(last_ready, s - 1)
                elif s >= 2:
                    dve.wait_ge(x2_ready, SUB * j + s - 1)
                dve.tensor_tensor(slot, aux(s + 1), bias[:], ALU.add).then_inc(out_biased, 1)
                dve.wait_ge(out_biased, SUB * j + s + 1)
                dve.tensor_tensor(slot, slot, gate[:, j // per_batch, :], ALU.mult)\
                   .then_inc(out_scaled, 1)

            def body(i, before, after):
                j = i - 1
                if before:
                    group_variance(j)
                    wide(j, 0)
                    wide(j, 1)
                mix_piece(i, 1, 0)
                hi_piece(i, 1, 0)
                mix_piece(i, 1, 1)
                if before:
                    wide(j, 2)
                    normalise(j, 0)
                    wide(j, 3)
                    normalise(j, 1)
                hi_piece(i, 1, 1)
                if before:
                    normalise(j, 2)
                    normalise(j, 3)
                    gate_y(j, 0)
                    gate_y(j, 1)
                mix_piece(i, 1, 2)
                mix_piece(i, 1, 3)
                hi_piece(i, 1, 2)
                if before:
                    gate_y(j, 2)
                hi_piece(i, 1, 3)
                if before:
                    gate_y(j, 3)
                if not before:
                    split_lo(2)
                input_and_use(i, 2, use_a)
                for s in range(SUB):
                    if before:
                        scale_output(j, s)
                    layer_norm_stats(i + 1, s)
                layer_norm_moments(i + 1)
                set_current(i + 1)
                input_and_use(i, 3, use_v)
                if not before:
                    dve.wait_ge(mod_done, 4)
                    gate_out(dve, gate[:], wmod_tile["gate"][:, 0:batches, :], gate_rows, batches,
                             gate_step)
                    dve.wait_ge(bias_in, 16)
                layer_norm(i + 1)
                if not before:
                    split_lo(4)
                input_and_use(i, 4, scan)
                if not before:
                    take_modulation(1)
                input_and_use(i, 5, use_r)
                if after:
                    for c in range(KC):
                        mix_piece(i + 1, 0, c)
                        hi_piece(i + 1, 0, c)

            dve.wait_ge(sig_ready, 1)
            dve.tensor_tensor(silu[:], cT[:], sig[:], ALU.mult).then_inc(silu_ready, 1)
            dve.wait_ge(const_in, 6 * 16)
            dve.wait_ge(const_set, 3)
            dve.tensor_scalar(unmix[:], mix[:], -1.0, 1.0, ALU.mult, ALU.add).then_inc(unmix_set, 1)
            dve.tensor_copy(center[:], center_in[:]).then_inc(unmix_set, 1)
            dve.wait_ge(unmix_set, 2)
            for s in range(SUB):
                layer_norm_stats(0, s)
            layer_norm_moments(0)
            take_modulation(0)
            set_current(0)
            layer_norm(0)
            dve.wait_ge(w_in[0], 16)
            for k in range(KC):
                dve.tensor_copy(w_hi[:, 0, k], w_raw[:, 0, k]).then_inc(w0_hi_set, 1)
            for c in range(KC):
                mix_piece(0, 0, c)
                hi_piece(0, 0, c)
            body(0, False, True)
            with dve.Fori(1, blocks - 1) as i:
                body(i, True, True)
            body(blocks - 1, True, False)
            group_variance(blocks - 1)
            wide(blocks - 1, 0)
            wide(blocks - 1, 1)
            for s in range(SUB):
                normalise(blocks - 1, s)
                if s + 2 < SUB:
                    wide(blocks - 1, s + 2)
            for c in range(KC):
                gate_y(blocks - 1, c)
            dve.wait_ge(x_in, 16 * (blocks + 2))
            for s in range(SUB):
                scale_output(blocks - 1, s)
                dve.wait_ge(out_scaled, SUB * (blocks - 1) + s + 1)
                dve.tensor_tensor(xt[:, s], xt[:, s], scaled[:, s % 2], ALU.add)\
                   .then_inc(last_ready, 1)

        @block.gpsimd
        def _(pool):
            def lo_piece(b, m, c):
                n = m * KC + c
                pool.wait_ge(hi_ready, PIECES * b + n + 1)
                pool.tensor_tensor(in_lo[:, n % HI_RING], mixed_in[:, n % F32_RING],
                                   in_hi[:, n % HI_RING].bitcast(F32), ALU.subtract)\
                    .then_inc(lo_ready, 1)

            def layer_norm_rstd(b):
                pool.wait_ge(ln_step, MOMENT_STEPS * (b + 1))
                pool.tensor_tensor(rstd[:], var_eps[:], half[:], ALU.pow)\
                    .then_inc(ln_rstd, 1)

            def split_lo(m):
                weight_lo(pool, w_hi_set, m, w_raw[:, m], w_hi[:, m], w_lo[:, m], w_ready[m])

            def y_lo_chunk(j, c):
                pool.wait_ge(y_hi_set, KC * j + c + 1)
                pool.tensor_tensor(y_lo[:, c, :], g_sig[:, c, :], y_hi[:, c, :].bitcast(F32),
                                   ALU.subtract).then_inc(y_lo_set, 1)

            def residual(j, s):
                pool.wait_ge(out_scaled, SUB * j + s + 1)
                pool.wait_ge(res_in[s % 2], 16 * (2 * j + s // 2 + 1))
                pool.tensor_tensor(res[:, s % 2], scaled[:, s % 2], res[:, s % 2], ALU.add)\
                    .then_inc(x2_ready, 1)

            def body(i, before, after):
                lo_piece(i, 1, 0)
                lo_piece(i, 1, 1)
                if before:
                    y_lo_chunk(i - 1, 0)
                    y_lo_chunk(i - 1, 1)
                lo_piece(i, 1, 2)
                if before:
                    y_lo_chunk(i - 1, 2)
                lo_piece(i, 1, 3)
                if before:
                    y_lo_chunk(i - 1, 3)
                for c in range(KC):
                    lo_piece(i, 2, c)
                if not before:
                    split_lo(3)
                if before:
                    for s in range(SUB):
                        residual(i - 1, s)
                layer_norm_rstd(i + 1)
                for m in (3, 4, 5):
                    if not before and m == 5:
                        split_lo(m)
                    for c in range(KC):
                        lo_piece(i, m, c)
                if after:
                    for c in range(KC):
                        lo_piece(i + 1, 0, c)
                if not before:
                    split_lo(NP)

            pool.memset(half[:], -0.5).then_inc(const_set, 1)
            pool.memset(state[:], 0.0).then_inc(const_set, 1)
            pool.memset(hT[:, :, 0:1], 0.0).then_inc(const_set, 1)
            pool.wait_ge(const_set, 3)
            layer_norm_rstd(0)
            for k in range(KC):
                weight_lo(pool, w0_hi_set, k + 1, w_raw[:, 0, k], w_hi[:, 0, k], w_lo[:, 0, k],
                          w_ready[0])
                if k > 0:
                    lo_piece(0, 0, k - 1)
            lo_piece(0, 0, KC - 1)
            split_lo(1)
            body(0, False, True)
            with pool.Fori(1, blocks - 1) as i:
                body(i, True, True)
            body(blocks - 1, True, False)
            for c in range(KC):
                y_lo_chunk(blocks - 1, c)


def feed_forward(nc, x2, out, w2, b1_in, b2, wmod, silu, modulation, hT, w1_raw, identity,
                 batches, seq):
    tokens = x2.shape[0]
    blocks = tokens // TOK
    per_batch = seq // TOK
    x2_view = x2.rearrange("(n p) d -> n p d", p=P)
    out_view = out.rearrange("(n p) d -> n p d", p=P)
    F2_STEPS = JC + SUB - 1
    LN_AT, T_AT, GATE_AT = 5, 9, 7

    with ExitStack() as ctx:
        def sb(name, shape, dt=F32):
            return ctx.enter_context(nc.sbuf_tensor(name, shape, dt))

        def sem(name):
            return ctx.enter_context(nc.semaphore(name))

        w1_lo = sb("w1_lo", [P, KC, INTER], F32R)
        w1_hi = sb("w1_hi", [P, KC, INTER], F32R)
        w2_hi = sb("w2_hi", [P, JC, D], F32R)
        w2_raw = under(nc, "w2_raw", [P, JC, D])
        w2_lo = sb("w2_lo", [P, JC, D], F32R)
        gate = sb("f_gate", [P, batches, D])
        bias = sb("f_bias", [P, D])
        wmod_gate = sb("f_wmod_gate", [P, KC, D])

        w2_view = w2.rearrange("(j p) n -> p j n", p=P)
        parts = []
        for q in range(JC // KC):
            cols, rows = slice(q * D, (q + 1) * D), slice(q * KC, (q + 1) * KC)
            parts += [(w1_raw[:, :, cols], w1_hi[:, :, cols], w1_lo[:, :, cols]),
                      (w2_raw[:, rows, :], w2_hi[:, rows, :], w2_lo[:, rows, :])]

        ident = sb("f_ident", [P, P])
        b1 = sb("b1", [P, JC])
        current = sb("f_current", [P, 2, KC])
        half = sb("f_half", [P, SUB])
        xt = sb("x2t", [P, 2, SUB, D])
        stats = sb("f_stats", [P, SUB, 6])
        mean = sb("f_mean", [P, SUB])
        scratch = sb("f_scratch", [P, 2, SUB])
        var_eps = sb("f_var_eps", [P, SUB])
        rstd = sb("f_rstd", [P, SUB])
        xn = sb("xn", [P, SUB, D])
        h_hi = sb("h_hi", [P, KC, TOK], F32R)
        h_lo = sb("h_lo", [P, KC, TOK], F32R)
        hid = sb("hid", [P, 2, TOK])
        hid_hi = sb("hid_hi", [P, 2, TOK], F32R)
        hid_lo = sb("hid_lo", [P, 2, TOK], F32R)
        ps = ctx.enter_context(nc.psum_tensor("f_ps", [P, 8, 512], F32))

        w2_in = [sem(f"w2_in{q}") for q in range(JC // KC)]
        w0_hi_set = sem("f_w0_hi_set")
        w_hi_set = sem("f_w_hi_set")
        w_ready = [sem(f"f_w_ready{n}") for n in range(len(parts))]
        wmod_in = sem("f_wmod_in")
        gate_done = sem("f_gate_done")
        gate_step = sem("f_gate_step")
        bias_in = sem("f_bias_in")
        current_set = sem("f_current_set")
        const_in = sem("f_const_in")
        half_set = sem("f_half_set")
        x2_in = sem("x2_in")
        stored = sem("stored")
        last_stored = [sem(f"last_stored{s}") for s in range(SUB)]
        ln_stats = sem("f_ln_stats")
        ln_step = sem("f_ln_step")
        ln_rstd = sem("f_ln_rstd")
        xn_ready = sem("f_xn_ready")
        t_done = sem("f_t_done")
        h_ready = sem("f_h_ready")
        h_hi_set = sem("h_hi_set")
        h_lo_set = sem("h_lo_set")
        up_done = sem("up_done")
        relu_done = sem("relu_done")
        hid_hi_set = sem("hid_hi_set")
        hid_lo_set = sem("hid_lo_set")
        down_step = sem("down_step")
        sum_biased = sem("sum_biased")
        sum_scaled = sem("sum_scaled")
        out_ready = sem("out_ready")

        def chunk_used(i, j):
            if j < 0:
                j, i = j + JC, i - 1
            return F2_STEPS * i + (j + 1 if j < JC - 1 else F2_STEPS)

        def sum_done(i, s):
            return F2_STEPS * i + JC + s

        up_bank = [ps[:, 0], ps[:, 1]]
        t_bank = [ps[:, 2], ps[:, 3]]
        sums = [ps[:, 4 + s] for s in range(SUB)]

        block = ctx.enter_context(nc.Block())

        @block.sync
        def _(sp):
            sp.dma_start(ident[:], identity).then_inc(const_in, 16)
            sp.dma_start(b1[:], b1_in).then_inc(const_in, 16)

            def load(b):
                wait(sp, stored, 16 * (b - 1))
                wait(sp, x2_in, 16 * b)
                sp.dma_start(xt[:, b % 2], x2_view[bass.ds(SUB * b, SUB)].rearrange("s p d -> p s d"))\
                  .then_inc(x2_in, 16)

            def store(b):
                sp.wait_ge(out_ready, SUB * (b + 1))
                sp.dma_start(out_view[bass.ds(SUB * b, SUB)].rearrange("s p d -> p s d"), xt[:, b % 2])\
                  .then_inc(stored, 16)

            for q in range(JC // KC):
                rows = slice(q * KC, (q + 1) * KC)
                sp.dma_start(w2_raw[:, rows, :], w2_view[:, rows, :]).then_inc(w2_in[q], 16)
                if q == 0:
                    load(0)
                    sp.dma_start(wmod_gate[:], wmod.rearrange("(k p) n -> p k n", p=P)[:, :, 5 * D:])\
                      .then_inc(wmod_in, 16)
                    sp.dma_start(bias[:], b2.partition_broadcast(P)).then_inc(bias_in, 16)
                    load(1)
            store(0)
            with sp.Fori(1, blocks - 1) as i:
                load(i + 1)
                store(i)
            for s in range(SUB):
                b = blocks - 1
                sp.wait_ge(out_ready, SUB * b + s + 1)
                sp.dma_start(out_view[SUB * b + s], xt[:, b % 2, s, :]).then_inc(last_stored[s], 16)
            sp.wait_ge(stored, 16 * (blocks - 1))
            for s in range(SUB):
                sp.wait_ge(last_stored[s], 16)

        @block.tensor
        def _(pe):
            def transpose_x(b, c):
                if c == 0:
                    pe.wait_ge(xn_ready, SUB * b)
                wait(pe, h_ready, KC * (b - 1) + c - 1)
                for s in range(SUB):
                    last = pe.transpose(t_bank[c % 2][:, s * P:(s + 1) * P],
                                        xn[:, s, c * P:(c + 1) * P], ident[:])
                last.then_inc(t_done, 1)

            def up(i, j):
                wait(pe, relu_done, JC * i + j - 1)
                cols = slice(j * P, (j + 1) * P)
                if isinstance(i, int) and i == 0 and j < KC:
                    pe.wait_ge(w_ready[0], j + 1)
                elif j % KC == 0 and isinstance(i, int) and i == 0:
                    pe.wait_ge(w_ready[j // KC * 2], 1)
                for k in range(KC):
                    if j == 0:
                        pe.wait_ge(h_lo_set, KC * i + k + 1)
                    last = split_product(pe, up_bank[j % 2], w1_hi[:, k, cols], w1_lo[:, k, cols],
                                         h_hi[:, k, :], h_lo[:, k, :], k == 0, k == KC - 1)
                last.then_inc(up_done, 1)

            def down(i, j):
                if j % KC == 0 and isinstance(i, int) and i == 0:
                    pe.wait_ge(w_ready[j // KC * 2 + 1], 1)
                pe.wait_ge(hid_lo_set, JC * i + j + 1)
                for s in range(SUB):
                    if j == 0:
                        wait(pe, sum_biased, SUB * (i - 1) + s + 1)
                    rows = slice(s * P, (s + 1) * P)
                    last = split_product(pe, sums[s], hid_hi[:, j % 2, rows],
                                         hid_lo[:, j % 2, rows], w2_hi[:, j, :], w2_lo[:, j, :],
                                         j == 0, j == JC - 1)
                    if j == JC - 1 or s == SUB - 1:
                        last.then_inc(down_step, 1)

            def body(i, after):
                for j in range(JC):
                    up(i, j)
                    if j == T_AT and isinstance(i, int) and i == 0:
                        pe.wait_ge(const_in, 32)
                        pe.wait_ge(gate_step, batches)
                    if after and T_AT <= j < T_AT + KC:
                        transpose_x(i + 1, j - T_AT)
                    if j >= 2:
                        down(i, j - 2)
                    if j == GATE_AT and isinstance(i, int) and i == 0:
                        pe.wait_ge(wmod_in, 16)
                        gate_product(pe, t_bank, wmod_gate, silu, batches, gate_done)
                down(i, JC - 2)
                down(i, JC - 1)

            body(0, True)
            with pe.Fori(1, blocks - 1) as i:
                body(i, True)
            body(blocks - 1, False)

        @block.scalar
        def _(act):
            def split_hi(n):
                raw, hi, _ = parts[n]
                if n % 2:
                    act.wait_ge(w2_in[n // 2], 16)
                act.activation(hi, raw, ACT.Copy).then_inc(w_hi_set, 1)

            def modulated(b, c):
                act.wait_ge(t_done, KC * (b - 1) + c + 1)
                if c == 0:
                    act.wait_ge(current_set, b)
                    act.wait_ge(h_lo_set, KC * b)
                act.activation(hT[:, c, 1:], t_bank[c % 2], ACT.Identity,
                               bias=current[:, 0, c:c + 1], scale=current[:, 1, c:c + 1])\
                   .then_inc(h_ready, 1)

            def relu(i, j):
                wait(act, hid_lo_set, JC * i + j - 1)
                act.wait_ge(up_done, JC * i + j + 1)
                act.activation(hid[:, j % 2], up_bank[j % 2], ACT.Relu, bias=b1[:, j:j + 1])\
                   .then_inc(relu_done, 1)

            def body(i, after):
                for j in range(JC):
                    relu(i, j)
                    if after and T_AT <= j < T_AT + KC:
                        modulated(i + 1, j - T_AT)
                    if isinstance(i, int) and i == 0 and j % KC >= 2 and j < JC - KC:
                        split_hi(j // KC * 2 + j % KC)

            act.wait_ge(const_in, 32)
            split_hi(1)
            body(0, True)
            with act.Fori(1, blocks - 1) as i:
                body(i, True)
            body(blocks - 1, False)

        @block.vector
        def _(dve):
            def layer_norm_stats(b):
                dve.tensor_scalar(current[:], modulation[:, 1, b // per_batch], 1.0, None, ALU.mult)\
                   .then_inc(current_set, 1)
                dve.wait_ge(x2_in, 16 * (b + 1))
                for s in range(SUB):
                    dve.bn_stats(stats[:, s, :], xt[:, b % 2, s, :]).then_inc(ln_stats, 1)
                dve.wait_ge(ln_stats, SUB * b)
                moments_steps(dve, ln_step, MOMENT_STEPS * (b - 1), stats, mean[:], var_eps[:],
                              scratch)

            def layer_norm(b):
                dve.wait_ge(ln_rstd, b)
                wait(dve, t_done, KC * (b - 1))
                for s in range(SUB):
                    dve.tensor_scalar(xn[:, s, :], xt[:, b % 2, s, :], mean[:, s:s + 1],
                                      rstd[:, s:s + 1], ALU.subtract, ALU.mult)\
                       .then_inc(xn_ready, 1)

            def split_h(b, chunks=range(KC)):
                wait(dve, up_done, JC * b)
                for c in chunks:
                    if not isinstance(b, int) or b > 0:
                        dve.wait_ge(h_ready, KC * (b - 1) + c + 1)
                    dve.tensor_copy(h_hi[:, c, :], hT[:, c, 1:]).then_inc(h_hi_set, 1)
                    dve.wait_ge(h_hi_set, KC * b + c + 1)
                    dve.tensor_tensor(h_lo[:, c, :], hT[:, c, 1:], h_hi[:, c, :].bitcast(F32),
                                      ALU.subtract).then_inc(h_lo_set, 1)

            def hidden_hi(i, j):
                dve.wait_ge(relu_done, JC * i + j + 1)
                wait(dve, down_step, chunk_used(i, j - 2) if j >= 2 or not isinstance(i, int)
                     or i > 0 else 0)
                dve.tensor_copy(hid_hi[:, j % 2], hid[:, j % 2]).then_inc(hid_hi_set, 1)

            def sum_out(i, s):
                dve.wait_ge(down_step, sum_done(i, s))
                dve.tensor_tensor(xn[:, s, :], sums[s], bias[:], ALU.add).then_inc(sum_biased, 1)

            def scale_sum(i, s):
                dve.wait_ge(sum_biased, SUB * i + s + 1)
                dve.tensor_tensor(xn[:, s, :], xn[:, s, :], gate[:, i // per_batch, :], ALU.mult)\
                   .then_inc(sum_scaled, 1)
                dve.wait_ge(sum_scaled, SUB * i + s + 1)
                part = xt[:, i % 2, s, :]
                dve.tensor_tensor(part, part, xn[:, s, :], ALU.add).then_inc(out_ready, 1)

            def split_lo(n):
                weight_lo(dve, w_hi_set, n, *parts[n], w_ready[n])

            def body(i, before, after):
                for j in range(JC):
                    hidden_hi(i, j)
                    if before and j < SUB:
                        scale_sum(i - 1, j)
                    if not before and j % KC >= 2 and j < JC - KC:
                        split_lo(j // KC * 2 + j % KC)
                    if not before and j == GATE_AT:
                        dve.wait_ge(gate_done, 1)
                        gate_out(dve, gate[:], wmod_gate[:, 0:batches, :], t_bank, batches,
                                 gate_step)
                        dve.wait_ge(bias_in, 16)
                    if after and j == LN_AT:
                        layer_norm_stats(i + 1)
                    if after and j == LN_AT + 1:
                        layer_norm(i + 1)
                if after:
                    split_h(i + 1)
                for s in range(SUB):
                    sum_out(i, s)
                    if not after:
                        scale_sum(i, s)

            for j in range(KC):
                cols = slice(j * P, (j + 1) * P)
                dve.tensor_copy(w1_hi[:, :, cols], w1_raw[:, :, cols]).then_inc(w0_hi_set, 1)
                split_h(0, (j,))
            split_lo(1)
            body(0, False, True)
            with dve.Fori(1, blocks - 1) as i:
                body(i, True, True)
            body(blocks - 1, True, False)

        @block.gpsimd
        def _(pool):
            def layer_norm_rstd(b):
                pool.wait_ge(ln_step, MOMENT_STEPS * b)
                pool.tensor_tensor(rstd[:], var_eps[:], half[:], ALU.pow).then_inc(ln_rstd, 1)

            def hidden_lo(i, j):
                pool.wait_ge(hid_hi_set, JC * i + j + 1)
                pool.tensor_tensor(hid_lo[:, j % 2], hid[:, j % 2], hid_hi[:, j % 2].bitcast(F32),
                                   ALU.subtract).then_inc(hid_lo_set, 1)

            def body(i, after):
                for j in range(JC):
                    hidden_lo(i, j)
                    if after and j == LN_AT:
                        layer_norm_rstd(i + 1)

            pool.memset(half[:], -0.5).then_inc(half_set, 1)
            pool.wait_ge(half_set, 1)
            for j in range(KC):
                cols = slice(j * P, (j + 1) * P)
                weight_lo(pool, w0_hi_set, j + 1, w1_raw[:, :, cols], w1_hi[:, :, cols],
                          w1_lo[:, :, cols], w_ready[0])
            body(0, True)
            with pool.Fori(1, blocks - 1) as i:
                body(i, True)
            body(blocks - 1, False)


def build(nc, a):
    batches, seq, _ = a["x"].shape
    flat = "b t d -> (b t) d"
    x2 = nc.dram_tensor("x2", (batches * seq, D), F32).ap()
    with ExitStack() as ctx:
        silu = ctx.enter_context(nc.sbuf_tensor("silu", [P, KC, batches], F32))
        modulation = ctx.enter_context(nc.sbuf_tensor("modulation", [P, 2, batches, 2, KC], F32))
        hT = ctx.enter_context(nc.sbuf_tensor("hT", [P, KC, 1 + TOK], F32))
        w1_raw = under(nc, "w1_raw", [P, KC, INTER])
        attention(nc, a["x"].rearrange(flat), x2, a["mix"], [a[f"W_{m}"] for m in PROJ],
                  a["W_out"], a["b_out"], a["gn"], a["cT"], a["wmod"],
                  a["W1"].rearrange("(k p) n -> p k n", p=P), silu, modulation, hT, w1_raw,
                  a["identity"], a["centering"], a["group_mean"], a["keep"], batches, seq)
        feed_forward(nc, x2, a["out"].rearrange(flat), a["W2"], a["b1"], a["b2"], a["wmod"],
                     silu, modulation, hT, w1_raw, a["identity"], batches, seq)


def kernel(**inputs):
    import numpy as np
    import concourse.bacc as bacc
    from concourse.bass_utils import run_bass_kernel_spmd

    def attn(name):
        return np.asarray(inputs[f"L0_attn_{name}"])

    def by_chunk(vector):
        return vector.reshape(-1, P).T

    x = attn("x")
    batches, seq, _ = x.shape
    arrays = {"x": x, "W1": inputs["L0_ffn_W1"], "W2": inputs["L0_ffn_W2"],
              "wmod": inputs["L0_wmod"], "W_out": attn("W_out").T}
    for m in PROJ:
        arrays[f"W_{m}"] = attn(f"W_{m}").T
    arrays["mix"] = np.concatenate([by_chunk(attn(f"x_{m}").reshape(D)) for m in PROJ], axis=1)
    arrays["gn"] = np.stack([by_chunk(attn("gn_w")), by_chunk(attn("gn_b"))], axis=1)
    arrays["cT"] = np.asarray(inputs["L0_c"]).T.reshape(KC, P, batches).transpose(1, 0, 2)
    arrays["b_out"] = attn("b_out").reshape(1, D)
    arrays["b1"] = by_chunk(np.asarray(inputs["L0_ffn_b1"]))
    arrays["b2"] = np.asarray(inputs["L0_ffn_b2"]).reshape(1, D)
    same = np.kron(np.eye(GPC), np.full((GROUP, GROUP), 1.0 / GROUP))
    keep = np.ones((P, batches * seq // TOK + 1))
    keep[:, ::seq // TOK] = 0.0
    arrays["identity"] = np.eye(P)
    arrays["centering"] = np.eye(P) - same
    arrays["group_mean"] = same[:, ::GROUP]
    arrays["keep"] = keep
    arrays = {n: np.ascontiguousarray(v, np.float32) for n, v in arrays.items()}

    nc = bacc.Bacc("TRN2", target_bir_lowering=False, num_devices=1)
    aps = {n: nc.dram_tensor(f"in_{n}", v.shape, F32, kind="ExternalInput").ap()
           for n, v in arrays.items()}
    aps["out"] = nc.dram_tensor("out", x.shape, F32, kind="ExternalOutput").ap()
    build(nc, aps)
    result = run_bass_kernel_spmd(nc, [{f"in_{n}": v for n, v in arrays.items()}], core_ids=[0])
    return result.results[0]["out"]
```
